# Optimizing a Trainium2 kernel written in Bass

```python
import numpy as np
import jax
import jax.numpy as jnp

def _softmax(x, axis=-1):
    return jax.nn.softmax(x, axis=axis)

def _gelu(x):
    return jax.nn.gelu(x, approximate=True)

def _silu(x):
    return jax.nn.silu(x)

def _sigmoid(x):
    return jax.nn.sigmoid(x)

def _layernorm(x, axis=-1, eps=1e-05):
    m = jnp.mean(x, axis=axis, keepdims=True)
    v = jnp.var(x, axis=axis, keepdims=True)
    return (x - m) / jnp.sqrt(v + eps)

def _scatter_add(tgt, idx, src, axis=0):
    return tgt.at[idx].add(src)

def _segment_sum(src, seg, n):
    return jax.ops.segment_sum(src, seg, n)
kernel_name = 'mk_gnn_preln_d2_gnn_r8_99bfd8'

def setup_inputs(seed: int=0):
    np.random.seed(seed)
    _w = jnp.asarray

    def _rec_inputs():
        import jax
        import jax.numpy as jnp
        _gk = jax.random.key(seed)
        x = 7.22e-05 + 1 * jax.random.normal(jax.random.fold_in(_gk, 1), (6250, 256), jnp.float32)
        src = jax.random.randint(jax.random.fold_in(_gk, 2), (100000,), 0, 6250, jnp.int32)
        dst = jax.random.randint(jax.random.fold_in(_gk, 3), (100000,), 0, 6250, jnp.int32)
        _o = jnp.argsort(dst, stable=True)
        src = src[_o]
        dst = dst[_o]
        edge_attr_128 = 9.41057e-06 + 1 * jax.random.normal(jax.random.fold_in(_gk, 11), (100000, 128), jnp.float32)
        node_vec1 = jax.random.uniform(jax.random.fold_in(_gk, 13), (6250, 1), jnp.float32, 0.0, 0.999973)
        node_vec1_n2 = jax.random.uniform(jax.random.fold_in(_gk, 14), (6250, 1), jnp.float32, 0.0, 0.999973)
        return (x, src, dst, edge_attr_128, node_vec1, node_vec1_n2)
    x, src, dst, edge_attr_128, node_vec1, node_vec1_n2 = _rec_inputs()

    def _L0_gnn_setup():
        import jax, jax.numpy as jnp
        import numpy as np
        import math
        N = 4096
        E = N * 16
        D = 256
        H = 8
        DH = 32
        TD = H * DH
        FFN = 1024
        L = 2
        EPS = 1e-05

        def _layernorm(x, g, b):
            mu = jnp.mean(x, axis=-1, keepdims=True)
            var = jnp.mean(jnp.square(x - mu), axis=-1, keepdims=True)
            return (x - mu) * jax.lax.rsqrt(var + EPS) * g + b
        key = jax.random.key(seed)
        ks = jax.random.split(key, 16)
        w = lambda k, *s: jax.random.normal(k, s, dtype=jnp.float32) * 0.02
        return {'x': jax.random.normal(ks[0], (N, D), dtype=jnp.float32), 'edge_index': jax.random.randint(ks[1], (2, E), 0, N, dtype=jnp.int64).astype(jnp.int32), 'w_in': w(ks[2], D, D), 'b_in': jnp.zeros((D,), jnp.float32), 'ln1_g': jnp.ones((L, D), jnp.float32), 'ln1_b': jnp.zeros((L, D), jnp.float32), 'ln2_g': jnp.ones((L, D), jnp.float32), 'ln2_b': jnp.zeros((L, D), jnp.float32), 'wq': w(ks[3], L, D, TD), 'bq': jnp.zeros((L, TD), jnp.float32), 'wk': w(ks[4], L, D, TD), 'bk': jnp.zeros((L, TD), jnp.float32), 'wv': w(ks[5], L, D, TD), 'bv': jnp.zeros((L, TD), jnp.float32), 'wo': w(ks[6], L, TD, D), 'bo': jnp.zeros((L, D), jnp.float32), 'w1': w(ks[7], L, D, FFN), 'b1': jnp.zeros((L, FFN), jnp.float32), 'w2': w(ks[8], L, FFN, D), 'b2': jnp.zeros((L, D), jnp.float32)}
    _L0_gnn_all = _L0_gnn_setup()
    _L0_gnn_in = {k: v for k, v in _L0_gnn_all.items() if k in ('w_in', 'b_in', 'ln1_g', 'ln1_b', 'ln2_g', 'ln2_b', 'wq', 'bq', 'wk', 'bk', 'wv', 'bv', 'wo', 'bo', 'w1', 'b1', 'w2', 'b2')}
    del _L0_gnn_all

    def _L1_gnn_setup():
        import jax, jax.numpy as jnp
        import numpy as np
        NUM_NODES = 6250
        NUM_EDGES = 200000
        NODE_DIM = 256
        EDGE_DIM = 128
        MAX_IN_DEGREE = 512
        MAX_OUT_DEGREE = 512
        key = jax.random.key(seed)
        ks = jax.random.split(key, 12)
        x = jax.random.normal(ks[0], (NUM_NODES, NODE_DIM), dtype=jnp.float32)
        edge_index = jax.random.randint(ks[1], (2, NUM_EDGES), 0, NUM_NODES, dtype=jnp.int64 if jax.config.read('jax_enable_x64') else jnp.int32)
        edge_attr = jax.random.normal(ks[2], (NUM_EDGES, EDGE_DIM), dtype=jnp.float32)
        voronoi_values = jax.random.uniform(ks[3], (NUM_NODES, 1), dtype=jnp.float32)
        centralities = jax.random.uniform(ks[4], (NUM_NODES, 1), dtype=jnp.float32)
        z_in = jax.random.normal(ks[5], (MAX_IN_DEGREE, NODE_DIM), dtype=jnp.float32)
        z_out = jax.random.normal(ks[6], (MAX_OUT_DEGREE, NODE_DIM), dtype=jnp.float32)
        W_cent = jax.random.normal(ks[7], (1, NODE_DIM), dtype=jnp.float32) * 0.5
        b_cent = jnp.zeros((NODE_DIM,), dtype=jnp.float32)
        W_vor = jax.random.normal(ks[8], (1, NODE_DIM), dtype=jnp.float32) * 0.5
        b_vor = jnp.zeros((NODE_DIM,), dtype=jnp.float32)
        W_sum = jax.random.normal(ks[9], (EDGE_DIM, NODE_DIM), dtype=jnp.float32) * (1.0 / np.sqrt(EDGE_DIM))
        b_sum = jnp.zeros((NODE_DIM,), dtype=jnp.float32)
        return {'x': x, 'edge_index': edge_index, 'edge_attr': edge_attr, 'voronoi_values': voronoi_values, 'centralities': centralities, 'z_in': z_in, 'z_out': z_out, 'W_cent': W_cent, 'b_cent': b_cent, 'W_vor': W_vor, 'b_vor': b_vor, 'W_sum': W_sum, 'b_sum': b_sum}
    _L1_gnn_all = _L1_gnn_setup()
    _L1_gnn_in = {k: v for k, v in _L1_gnn_all.items() if k in ('z_in', 'z_out', 'W_cent', 'b_cent', 'W_vor', 'b_vor', 'W_sum', 'b_sum')}
    del _L1_gnn_all
    return {'x': x, 'src': src, 'dst': dst, 'edge_attr_128': edge_attr_128, 'node_vec1': node_vec1, 'node_vec1_n2': node_vec1_n2, 'L0_gnn_w_in': _L0_gnn_in['w_in'], 'L0_gnn_b_in': _L0_gnn_in['b_in'], 'L0_gnn_ln1_g': _L0_gnn_in['ln1_g'], 'L0_gnn_ln1_b': _L0_gnn_in['ln1_b'], 'L0_gnn_ln2_g': _L0_gnn_in['ln2_g'], 'L0_gnn_ln2_b': _L0_gnn_in['ln2_b'], 'L0_gnn_wq': _L0_gnn_in['wq'], 'L0_gnn_bq': _L0_gnn_in['bq'], 'L0_gnn_wk': _L0_gnn_in['wk'], 'L0_gnn_bk': _L0_gnn_in['bk'], 'L0_gnn_wv': _L0_gnn_in['wv'], 'L0_gnn_bv': _L0_gnn_in['bv'], 'L0_gnn_wo': _L0_gnn_in['wo'], 'L0_gnn_bo': _L0_gnn_in['bo'], 'L0_gnn_w1': _L0_gnn_in['w1'], 'L0_gnn_b1': _L0_gnn_in['b1'], 'L0_gnn_w2': _L0_gnn_in['w2'], 'L0_gnn_b2': _L0_gnn_in['b2'], 'L1_gnn_z_in': _L1_gnn_in['z_in'], 'L1_gnn_z_out': _L1_gnn_in['z_out'], 'L1_gnn_W_cent': _L1_gnn_in['W_cent'], 'L1_gnn_b_cent': _L1_gnn_in['b_cent'], 'L1_gnn_W_vor': _L1_gnn_in['W_vor'], 'L1_gnn_b_vor': _L1_gnn_in['b_vor'], 'L1_gnn_W_sum': _L1_gnn_in['W_sum'], 'L1_gnn_b_sum': _L1_gnn_in['b_sum']}

def reference(x, src, dst, edge_attr_128, node_vec1, node_vec1_n2, L0_gnn_w_in, L0_gnn_b_in, L0_gnn_ln1_g, L0_gnn_ln1_b, L0_gnn_ln2_g, L0_gnn_ln2_b, L0_gnn_wq, L0_gnn_bq, L0_gnn_wk, L0_gnn_bk, L0_gnn_wv, L0_gnn_bv, L0_gnn_wo, L0_gnn_bo, L0_gnn_w1, L0_gnn_b1, L0_gnn_w2, L0_gnn_b2, L1_gnn_z_in, L1_gnn_z_out, L1_gnn_W_cent, L1_gnn_b_cent, L1_gnn_W_vor, L1_gnn_b_vor, L1_gnn_W_sum, L1_gnn_b_sum):
    import jax
    import jax.numpy as jnp

    def _L0_gnn_ref(x, edge_index, w_in, b_in, ln1_g, ln1_b, ln2_g, ln2_b, wq, bq, wk, bk, wv, bv, wo, bo, w1, b1, w2, b2):
        import jax, jax.numpy as jnp
        import numpy as np
        import math
        N = 4096
        E = N * 16
        D = 256
        H = 8
        DH = 32
        TD = H * DH
        FFN = 1024
        L = 2
        EPS = 1e-05

        def _layernorm(x, g, b):
            mu = jnp.mean(x, axis=-1, keepdims=True)
            var = jnp.mean(jnp.square(x - mu), axis=-1, keepdims=True)
            return (x - mu) * jax.lax.rsqrt(var + EPS) * g + b
        n = x.shape[0]
        src0, dst0 = (edge_index[0], edge_index[1])
        deg = jax.ops.segment_sum(jnp.ones_like(src0, jnp.float32), dst0, num_segments=n)
        ar = jnp.arange(n, dtype=src0.dtype)
        src = jnp.concatenate([src0, ar])
        dst = jnp.concatenate([dst0, ar])
        h = x @ w_in + b_in
        scale = 1.0 / math.sqrt(DH)
        for l in range(L):
            xn = _layernorm(h, ln1_g[l], ln1_b[l])
            q = (xn @ wq[l] + bq[l]).reshape(n, H, DH)
            k = (xn @ wk[l] + bk[l]).reshape(n, H, DH)
            v = (xn @ wv[l] + bv[l]).reshape(n, H, DH)
            scores = jnp.einsum('ehd,ehd->eh', q[dst], k[src]) * scale
            m = jax.ops.segment_max(scores, dst, num_segments=n)
            ex = jnp.exp(scores - m[dst])
            z = jax.ops.segment_sum(ex, dst, num_segments=n)
            attn = ex / z[dst]
            agg = jax.ops.segment_sum(attn[:, :, None] * v[src], dst, num_segments=n)
            agg = jnp.where((deg > 0)[:, None, None], agg, 0.0)
            h = h + agg.reshape(n, TD) @ wo[l] + bo[l] * jnp.where(deg > 0, 1.0, 1.0)[:, None] * 0 + agg.reshape(n, TD) @ wo[l] * 0
            h = h - agg.reshape(n, TD) @ wo[l]
            h = h + (agg.reshape(n, TD) @ wo[l] + bo[l]) - bo[l] * 0
            xn2 = _layernorm(h, ln2_g[l], ln2_b[l])
            ffn = jax.nn.gelu(xn2 @ w1[l] + b1[l], approximate=False) @ w2[l] + b2[l]
            h = h + ffn
        return h

    def _L1_gnn_ref(x, edge_index, edge_attr, voronoi_values, centralities, z_in, z_out, W_cent, b_cent, W_vor, b_vor, W_sum, b_sum):
        import jax, jax.numpy as jnp
        import numpy as np
        NUM_NODES = 6250
        NUM_EDGES = 200000
        NODE_DIM = 256
        EDGE_DIM = 128
        MAX_IN_DEGREE = 512
        MAX_OUT_DEGREE = 512
        num_nodes = x.shape[0]
        src = edge_index[0]
        dst = edge_index[1]
        ones = jnp.ones_like(src, dtype=jnp.int32)
        in_deg = jnp.minimum(jax.ops.segment_sum(ones, dst, num_segments=num_nodes), MAX_IN_DEGREE - 1)
        out_deg = jnp.minimum(jax.ops.segment_sum(ones, src, num_segments=num_nodes), MAX_OUT_DEGREE - 1)
        edge_proj = edge_attr @ W_sum + b_sum
        sum3d = jax.ops.segment_sum(edge_proj, src, num_segments=num_nodes)
        cent_term = jax.nn.sigmoid(centralities @ W_cent + b_cent)
        vor_term = jax.nn.sigmoid(voronoi_values @ W_vor + b_vor)
        return x + z_in[in_deg] + z_out[out_deg] + cent_term + vor_term + sum3d
    edge_index = jnp.stack([src, dst])
    h = jnp.maximum(_layernorm(x, axis=-1), 0.0)
    x = x + _L0_gnn_ref(h, edge_index, L0_gnn_w_in, L0_gnn_b_in, L0_gnn_ln1_g, L0_gnn_ln1_b, L0_gnn_ln2_g, L0_gnn_ln2_b, L0_gnn_wq, L0_gnn_bq, L0_gnn_wk, L0_gnn_bk, L0_gnn_wv, L0_gnn_bv, L0_gnn_wo, L0_gnn_bo, L0_gnn_w1, L0_gnn_b1, L0_gnn_w2, L0_gnn_b2)
    h = jnp.maximum(_layernorm(x, axis=-1), 0.0)
    x = x + _L1_gnn_ref(h, edge_index, edge_attr_128, node_vec1, node_vec1_n2, L1_gnn_z_in, L1_gnn_z_out, L1_gnn_W_cent, L1_gnn_b_cent, L1_gnn_W_vor, L1_gnn_b_vor, L1_gnn_W_sum, L1_gnn_b_sum)
    return x

_drawn_inputs = setup_inputs


def setup_inputs(seed=0):
    import zlib

    import numpy as np

    out = dict(_drawn_inputs(seed))
    spreads = {'L0_gnn_b_in': (0.0, 0.1),
     'L0_gnn_ln1_g': (1.0, 0.6),
     'L0_gnn_ln1_b': (0.0, 0.8),
     'L0_gnn_ln2_g': (1.0, 0.6),
     'L0_gnn_ln2_b': (0.0, 0.8),
     'L0_gnn_bq': (0.0, 2.0),
     'L0_gnn_bk': (0.0, 2.0),
     'L0_gnn_bv': (0.0, 0.529),
     'L0_gnn_bo': (0.0, 0.1),
     'L0_gnn_b1': (0.0, 0.468),
     'L0_gnn_b2': (0.0, 0.1),
     'L1_gnn_b_cent': (0.0, 2.0),
     'L1_gnn_b_vor': (0.0, 2.0),
     'L1_gnn_b_sum': (0.0, 0.1)}
    factors = {'node_vec1': 8.0,
     'node_vec1_n2': 8.0,
     'L0_gnn_wq': 8.0,
     'L0_gnn_wk': 8.0,
     'L1_gnn_W_cent': 4.019,
     'L1_gnn_W_vor': 4.273}
    for name, (base, spread) in spreads.items():
        noise = np.random.default_rng([zlib.crc32(name.encode()), seed]).standard_normal(out[name].shape)
        drawn = base * np.exp(spread * noise) if base else spread * noise
        out[name] = jnp.asarray(drawn.astype(out[name].dtype))
    for name, factor in factors.items():
        out[name] = (out[name] * factor).astype(out[name].dtype)
    return out
```

```python
import concourse.bass as bass
from concourse import mybir
from contextlib import ExitStack

f32 = mybir.dt.float32
bf16 = mybir.dt.bfloat16
i32 = mybir.dt.int32
ALU = mybir.AluOpType
ACT = mybir.ActivationFunctionType
AX = mybir.AxisListType

P = 128
N = 6250
E = 100000
D = 256
H = 8
DH = D // H
FF = 1024
L = 2
ED = 128
EPS = 1e-5
SCALE = float(DH) ** -0.5
MAX_DEG = 511

ET = -(-E // P)
LAST = E - 1 - (ET - 1) * P
NT = 50
NTA = NT + 4
NP = NT * P
NPA = NTA * P
PAIRS = NT // 2
CH = P // H
GI = 16
TURNS = 52
NI = GI * TURNS
IC = -(-NI // P)
HALF = GI // 2
QT = GI // 4
IG = NI // CH
SL = IG * P
BIG = 2.0 ** 126
QW = D + H
XW = D + 2 * H + 2
EG = 8
GROUPS = L * NT
YW = ED + 4
TABLES = 4
DUMMY = NP - P
SENTINEL = 1 << 20
assert NI >= ET + -(-N // P) - 1 and NI == CH * IG and GROUPS * EG * P >= E
assert NI - 1 - ET < NT and DUMMY >= N


class Names:

    def __init__(self, pool):
        self.pool = list(pool)

    def one(self):
        return self.pool.pop(0)

    def many(self, n):
        return [self.pool.pop(0) for _ in range(n)]


def gnn_kernel(nc, x, src_items, dst_items, src_rows, src_cols, edge_attr, vor_v, cent_v,
               w_in, b_in, ln1_g, ln1_b, ln2_g, ln2_b, wq, bq, wk, bk, wv, bv, wo, bo,
               w1, b1, w2, b2, z_in, z_out, w_cent, b_cent, w_vor, b_vor, w_sum, b_sum, out):
    Hd = nc.dram_tensor("h_scratch", [NPA, D], f32).ap()
    Kd = nc.dram_tensor("k_scratch", [NPA, D], f32).ap()
    Vd = nc.dram_tensor("v_scratch", [NPA, D], f32).ap()
    drel_d = nc.dram_tensor("drel_scratch", [IC * P * P], f32).ap()
    key_d = nc.dram_tensor("key_scratch", [IC * P * P + 1], f32).ap()
    nt_d = nc.dram_tensor("nt_scratch", [IC * P], i32).ap()
    sum_d = [nc.dram_tensor(f"sum_scratch{r}", [NP, YW], f32).ap() for r in range(TABLES)]

    ctx = ExitStack()
    pool = [ctx.enter_context(nc.semaphore(f"sem{n}")) for n in range(96)]
    rows_in = ctx.enter_context(nc.semaphore("rows_in"))
    ring_in = [ctx.enter_context(nc.semaphore(f"ring_in{n}")) for n in range(GI)]
    sc_s = [[ctx.enter_context(nc.semaphore(f"scatter{k}_{r}")) for r in range(TABLES)] for k in range(2)]
    zi_s = [ctx.enter_context(nc.semaphore(f"z_in{k}")) for k in range(2)]

    phase = [0]

    def sb(where, name, shape, dt=f32):
        return where.enter_context(nc.sbuf_tensor(f"{name}_{phase[0]}", shape, dt))

    def pb(where, name):
        return where.enter_context(nc.psum_tensor(f"{name}_{phase[0]}", [P, 512], f32))

    def end_phase():
        nc.gpsimd.sem_clear(range(pool[0].num, pool[-1].num + 1))
        nc.all_engine_barrier()
        phase[0] += 1

    with ctx:
        ident = sb(ctx, "ident", [P, P])
        iota_f = sb(ctx, "iota_f", [P, P])
        iota_p = sb(ctx, "iota_p", [P, 1])
        tril = sb(ctx, "tril", [P, P])
        neghalf = sb(ctx, "neghalf", [P, 1])
        ones = sb(ctx, "ones", [P, P])
        drel_c = sb(ctx, "drel_c", [P, IC * P])
        src_c = sb(ctx, "src_c", [P, IC * P], i32)
        nt_row = sb(ctx, "nt_row", [1, IC * P], i32)
        reset_f = sb(ctx, "reset_f", [P, SL], bf16)
        reset_b = sb(ctx, "reset_b", [P, SL], bf16)
        chain_f = sb(ctx, "chain_f", [1, P])
        chain_b = sb(ctx, "chain_b", [1, P])
        region = sb(ctx, "region", [P, 3 * SL])

        with ExitStack() as ph:
            last_i = sb(ph, "last_i", [1, ET], i32)
            last_h = sb(ph, "last_h", [1, ET], i32)
            last_f = sb(ph, "last_f", [1, ET])
            tile_no = sb(ph, "tile_no", [1, ET])
            bound = sb(ph, "bound", [1, ET])
            bound_b = sb(ph, "bound_b", [P, ET])
            junk = sb(ph, "junk", [P, ET])
            item_no = sb(ph, "item_no", [P, IC])
            et = sb(ph, "et", [P, IC])
            nt = sb(ph, "nt", [P, IC])
            base = sb(ph, "base", [P, IC])
            et_i = sb(ph, "et_i", [P, IC], i32)
            nt_i = sb(ph, "nt_i", [P, IC], i32)
            drow = sb(ph, "drow", [P, IC, P], i32)
            srow = sb(ph, "srow", [P, IC, P], i32)
            srow_f = sb(ph, "srow_f", [P, IC, P])
            drel = sb(ph, "drel", [P, IC, P])
            ge0 = sb(ph, "ge0", [P, IC, P])
            valid = sb(ph, "valid", [P, IC, P])
            key = sb(ph, "key", [P, IC, P])
            guard = sb(ph, "guard", [1, 1])
            zero = sb(ph, "zero", [P, (NTA - NT) * D])
            b0, b1_, tr0, tr1 = pb(ph, "b0"), pb(ph, "b1_"), pb(ph, "tr0"), pb(ph, "tr1")
            s = Names(pool)
            last_in, consts, sel_base, bound_done, bc_done, tables = s.many(6)
            drel_done, key_done, srcf_done, tr_done, tr_out, stored, nt_stored, nt_in, dve_c, zeroed, z_out_s = s.many(11)
            half = ET // 2
            with nc.Block() as block:
                @block.sync
                def _(sp):
                    sp.dma_start(last_i[0:1, 0:ET - 1],
                                 dst_items[0:ET - 1, P - 1:P].rearrange("t o -> o t"),
                                 allow_slow_non_contiguous=True).then_inc(last_in, 16)
                    sp.dma_start(last_i[0:1, ET - 1:ET],
                                 dst_items[ET - 1:ET, LAST:LAST + 1]).then_inc(last_in, 16)
                    sp.wait_ge(zeroed, 1)
                    for d in (Hd, Kd, Vd):
                        sp.dma_start(d[NP:NPA, :].rearrange("(p a) d -> p (a d)", p=P),
                                     zero[:, :]).then_inc(z_out_s, 16)
                    sp.wait_ge(tables, 2)
                    sp.dma_start(nt_d.rearrange("(c p) -> p c", p=P), nt_i[:, :],
                                 allow_slow_non_contiguous=True).then_inc(nt_stored, 16)
                    sp.wait_ge(nt_stored, 16)
                    sp.dma_start(nt_row[0:1, :], nt_d.rearrange("(a n) -> a n", a=1)).then_inc(nt_in, 16)
                    sp.wait_ge(drel_done, 1)
                    sp.dma_start(drel_d.rearrange("(c p e) -> p c e", p=P, e=P), drel[:, :, :]).then_inc(stored, 16)
                    sp.wait_ge(key_done, 1)
                    sp.dma_start(key_d[1:1 + IC * P * P].rearrange("(c p e) -> p c e", p=P, e=P),
                                 key[:, :, :]).then_inc(stored, 16)
                    sp.dma_start(key_d[0:1].rearrange("(a n) -> a n", a=1), guard[:, :]).then_inc(stored, 16)
                    sp.wait_ge(nt_in, 16)
                    sp.wait_ge(stored, 48)
                    sp.wait_ge(z_out_s, 48)

                @block.gpsimd
                def _(g):
                    g.memset(ident[:, :], 0.0).then_inc(sel_base, 1)
                    g.memset(tril[:, :], 1.0).then_inc(sel_base, 1)
                    g.memset(ones[:, :], 1.0)
                    g.memset(neghalf[:, :], -0.5)
                    g.memset(guard[:, :], -1.0)
                    g.iota(iota_f[:, :], [[1, P]], base=0, channel_multiplier=0,
                           allow_small_or_imprecise_dtypes=True)
                    g.iota(iota_p[:, :], [[0, 1]], base=0, channel_multiplier=1,
                           allow_small_or_imprecise_dtypes=True)
                    g.iota(tile_no[:, :], [[1, ET]], base=0, channel_multiplier=0,
                           allow_small_or_imprecise_dtypes=True)
                    g.iota(item_no[:, :], [[P, IC]], base=0, channel_multiplier=1,
                           allow_small_or_imprecise_dtypes=True)
                    g.wait_ge(sel_base, 2)
                    g.affine_select(out=ident[:, :], in_=ident[:, :], compare_op=ALU.not_equal, fill=1.0,
                                    base=0, pattern=[[-1, P]], channel_multiplier=1)
                    g.affine_select(out=tril[:, :], in_=tril[:, :], compare_op=ALU.is_gt, fill=0.0,
                                    base=0, pattern=[[-1, P]], channel_multiplier=1).then_inc(consts, 1)
                    g.wait_ge(tables, 1)
                    for c in range(IC):
                        off = bass.IndirectOffsetOnAxis(ap=et_i[:, c:c + 1], axis=0)
                        g.indirect_dma_start(out=drow[:, c, :], out_offset=None, in_=dst_items,
                                             in_offset=off).then_inc(rows_in, 16)
                        g.indirect_dma_start(out=srow[:, c, :], out_offset=None, in_=src_items,
                                             in_offset=off).then_inc(rows_in, 16)
                    g.wait_ge(rows_in, 32 * IC)

                @block.vector
                def _(v):
                    v.memset(zero[:, :], 0.0).then_inc(zeroed, 1)
                    v.wait_ge(last_in, 32)
                    v.tensor_scalar(out=last_h[:, :], in0=last_i[:, :], scalar1=7, scalar2=None,
                                    op0=ALU.arith_shift_right).then_inc(dve_c, 1)
                    v.wait_ge(dve_c, 1)
                    v.tensor_copy(last_f[:, :], last_h[:, :]).then_inc(dve_c, 1)
                    v.wait_ge(dve_c, 2)
                    v.wait_ge(consts, 1)
                    v.tensor_tensor(out=bound[:, :], in0=last_f[:, :], in1=tile_no[:, :],
                                    op=ALU.add).then_inc(bound_done, 1)
                    v.wait_ge(bc_done, 1)
                    v.tensor_copy(bound_b[:, 0:half], b0[:, 0:half])
                    v.tensor_copy(bound_b[:, half:ET], b1_[:, 0:ET - half]).then_inc(dve_c, 1)
                    v.wait_ge(dve_c, 3)
                    for c in range(IC):
                        if c >= 1:
                            v.wait_ge(dve_c, 3 + c)
                        v.tensor_scalar(out=junk[:, :], in0=bound_b[:, :], scalar1=item_no[:, c:c + 1],
                                        scalar2=None, op0=ALU.is_lt, op1=ALU.add,
                                        accum_out=et[:, c:c + 1]).then_inc(dve_c, 1)
                    v.wait_ge(dve_c, 3 + IC)
                    v.tensor_copy(et_i[:, :], et[:, :]).then_inc(tables, 1)
                    v.tensor_tensor(out=nt[:, :], in0=item_no[:, :], in1=et[:, :],
                                    op=ALU.subtract).then_inc(dve_c, 1)
                    v.wait_ge(dve_c, 4 + IC)
                    v.tensor_scalar(out=base[:, :], in0=nt[:, :], scalar1=float(P), scalar2=None,
                                    op0=ALU.mult).then_inc(dve_c, 1)
                    v.tensor_scalar(out=nt_i[:, :], in0=nt[:, :], scalar1=float(NT - 1), scalar2=None,
                                    op0=ALU.min).then_inc(tables, 1)
                    v.wait_ge(dve_c, 5 + IC)
                    v.wait_ge(rows_in, 32 * IC)
                    for c in range(IC):
                        ins = v.tensor_scalar(out=drel[:, c, :], in0=drow[:, c, :], scalar1=base[:, c:c + 1],
                                              scalar2=None, op0=ALU.subtract)
                    ins.then_inc(drel_done, 1)
                    v.tensor_copy(srow_f[:, :, :], srow[:, :, :]).then_inc(srcf_done, 1)
                    v.wait_ge(drel_done, 1)
                    v.tensor_scalar(out=ge0[:, :, :], in0=drel[:, :, :], scalar1=0.0, scalar2=None,
                                    op0=ALU.is_ge).then_inc(dve_c, 1)
                    v.wait_ge(dve_c, 6 + IC)
                    v.scalar_tensor_tensor(out=valid[:, :, :], in0=drel[:, :, :], scalar=float(P),
                                           in1=ge0[:, :, :], op0=ALU.is_lt, op1=ALU.mult).then_inc(dve_c, 1)
                    v.wait_ge(dve_c, 7 + IC)
                    v.scalar_tensor_tensor(out=key[:, :, :], in0=drow[:, :, :], scalar=1.0,
                                           in1=valid[:, :, :], op0=ALU.add, op1=ALU.mult).then_inc(key_done, 1)
                    for c in range(IC):
                        v.wait_ge(tr_done, c + 1)
                        cols = slice(c * P, (c + 1) * P)
                        v.tensor_copy(drel_c[:, cols], (tr0, tr1)[c % 2][:, 0:P])
                        v.tensor_copy(src_c[:, cols], (tr0, tr1)[c % 2][:, P:2 * P]).then_inc(tr_out, 1)

                @block.tensor
                def _(pe):
                    pe.wait_ge(consts, 1)
                    pe.wait_ge(bound_done, 1)
                    pe.matmul(b0[:, 0:half], ones[0:1, :], bound[0:1, 0:half], start=True, stop=True)
                    pe.matmul(b1_[:, 0:ET - half], ones[0:1, :], bound[0:1, half:ET],
                              start=True, stop=True).then_inc(bc_done, 1)
                    pe.wait_ge(drel_done, 1)
                    pe.wait_ge(srcf_done, 1)
                    for c in range(IC):
                        if c >= 2:
                            pe.wait_ge(tr_out, c - 1)
                        bank = (tr0, tr1)[c % 2]
                        pe.transpose(bank[:, 0:P], drel[:, c, :], ident[:, :])
                        pe.transpose(bank[:, P:2 * P], srow_f[:, c, :], ident[:, :]).then_inc(tr_done, 1)
            end_phase()

        with ExitStack() as ph:
            cur = region[:, 0:SL]
            prv = region[:, SL:2 * SL]
            nxt = region[:, 2 * SL:3 * SL]
            has_f = sb(ph, "has_f", [P, 1])
            has_b = sb(ph, "has_b", [P, 1])
            zeros = sb(ph, "zeros", [P, 10 * YW])
            cp = pb(ph, "cp")
            s = Names(pool)
            keys_in, ne, flags, red, trn, zr, z_done = s.many(7)
            with nc.Block() as block:
                @block.sync
                def _(sp):
                    for buf, at in ((cur, 1), (prv, 0), (nxt, 2)):
                        for h in range(H):
                            sp.dma_start(buf[h * CH:(h + 1) * CH, :],
                                         key_d[at:at + CH * SL].rearrange("(c j) -> c j", c=CH)).then_inc(keys_in, 16)
                    sp.wait_ge(zr, 1)
                    for r in range(TABLES):
                        for q in range(5):
                            sp.dma_start(sum_d[r][q * 10 * P:(q + 1) * 10 * P, :].rearrange("(p a) w -> p (a w)", p=P),
                                         zeros[:, :]).then_inc(z_done, 16)
                    sp.wait_ge(z_done, 16 * 5 * TABLES)

                @block.vector
                def _(v):
                    v.memset(zeros[:, :], 0.0).then_inc(zr, 1)
                    v.wait_ge(keys_in, 16 * 3 * H)
                    v.tensor_tensor(out=prv, in0=cur, in1=prv, op=ALU.not_equal).then_inc(ne, 1)
                    v.tensor_tensor(out=nxt, in0=cur, in1=nxt, op=ALU.not_equal).then_inc(ne, 1)
                    v.wait_ge(ne, 1)
                    v.tensor_scalar(out=reset_f[:, :], in0=prv, scalar1=-BIG, scalar2=None, op0=ALU.mult).then_inc(flags, 1)
                    v.wait_ge(ne, 2)
                    v.tensor_scalar(out=reset_b[:, :], in0=nxt, scalar1=-BIG, scalar2=None, op0=ALU.mult).then_inc(flags, 1)
                    v.wait_ge(flags, 1)
                    v.tensor_reduce(out=has_f[:, :], in_=reset_f[:, :], axis=AX.X, op=ALU.min).then_inc(red, 1)
                    v.wait_ge(flags, 2)
                    v.tensor_reduce(out=has_b[:, :], in_=reset_b[:, :], axis=AX.X, op=ALU.min).then_inc(red, 1)
                    v.wait_ge(trn, 1)
                    v.tensor_copy(chain_f[:, :], cp[0:1, 0:P])
                    v.tensor_copy(chain_b[:, :], cp[0:1, P:2 * P]).then_inc(red, 1)
                    v.wait_ge(red, 3)
                    v.memset(chain_f[0:1, 0:P:CH], -BIG)
                    v.memset(chain_b[0:1, CH - 1:P:CH], -BIG)

                @block.tensor
                def _(pe):
                    pe.wait_ge(red, 2)
                    pe.transpose(cp[0:1, 0:P], has_f[:, :], ident[:, :])
                    pe.transpose(cp[0:1, P:2 * P], has_b[:, :], ident[:, :]).then_inc(trn, 1)
            end_phase()
        def rows(d, n):
            return d[bass.ds(n * P, P), :]

        def project(l):
            first = l < 0
            W = D if first else 3 * D
            src = x if first else Hd
            with ExitStack() as ph:
                w = sb(ph, "w", [P, 2, W])
                bias = sb(ph, "bias", [P, W])
                gcol = sb(ph, "gcol", [P, 2])
                bcol = sb(ph, "bcol", [P, 2])
                bmat = sb(ph, "bmat", [P, 2, P])
                hin = sb(ph, "hin", [P, 2, D])
                st = sb(ph, "st", [P, 2, 6])
                mv = sb(ph, "mv", [P, 2, 2])
                veps = sb(ph, "veps", [P, 2, 1])
                rs = sb(ph, "rs", [P, 2, 1])
                xn = sb(ph, "xn", [P, 2, D])
                xT = sb(ph, "xT", [P, 2, D])
                res = sb(ph, "res", [P, 2, W])
                qk = sb(ph, "qk", [P, 2, D])
                tp = [pb(ph, f"tp{k}") for k in range(2)]
                mma = [pb(ph, f"mma{k}") for k in range(2)]
                mmb = [pb(ph, f"mmb{k}") for k in range(2)]
                s = Names(pool)
                w_in_s, bm, wf, bias_mm, bias_ok, aggr_go = s.many(6)
                h_in, st_s, mv_s, ve_s, rs_s, xn_s, tr_s, xt_s, mm_s, ev_s, pr_s, rd_s, kv_out = (s.many(2) for _ in range(13))

                with nc.Block() as block:
                    @block.sync
                    def _(sp):
                        if first:
                            sp.dma_start(w[:, :, :], w_in.rearrange("(c p) n -> p c n", p=P)).then_inc(w_in_s, 16)
                            sp.dma_start(bias[:, :], b_in.rearrange("(a n) -> a n", a=1).to_broadcast([P, D])).then_inc(w_in_s, 16)
                        else:
                            for j, (m, b) in enumerate(((wq, bq), (wk, bk), (wv, bv))):
                                cols = slice(j * D, (j + 1) * D)
                                sp.dma_start(w[:, :, cols], m[l].rearrange("(c p) n -> p c n", p=P)).then_inc(w_in_s, 16)
                                sp.dma_start(bias[:, cols], b[l:l + 1, :].to_broadcast([P, D])).then_inc(w_in_s, 16)
                            sp.dma_start(gcol[:, :], ln1_g[l].rearrange("(c p) -> p c", p=P),
                                         allow_slow_non_contiguous=True).then_inc(w_in_s, 16)
                            sp.dma_start(bcol[:, :], ln1_b[l].rearrange("(c p) -> p c", p=P),
                                         allow_slow_non_contiguous=True).then_inc(w_in_s, 16)
                        with sp.Fori(0, PAIRS) as t:
                            for k in range(2):
                                sp.wait_ge(ev_s[k], t + 1)
                                if first:
                                    sp.dma_start(rows(Hd, t * 2 + k), res[:, k, :]).then_inc(kv_out[k], 16)
                                else:
                                    sp.dma_start(rows(Kd, t * 2 + k), res[:, k, D:2 * D]).then_inc(kv_out[k], 16)
                                    sp.dma_start(rows(Vd, t * 2 + k), res[:, k, 2 * D:3 * D]).then_inc(kv_out[k], 16)
                        for k in range(2):
                            sp.wait_ge(kv_out[k], (16 if first else 32) * PAIRS)

                    def load(a, t, k):
                        a.wait_ge(xn_s[k], t)
                        a.dma_start(hin[:, k, :], rows(src, t * 2 + k)).then_inc(h_in[k], 16)

                    @block.scalar
                    def _(a):
                        def turned(t, k):
                            a.wait_ge(tr_s[k], t + 1)
                            a.wait_ge(mm_s[k], t)
                            a.activation(xT[:, k, :], tp[k][:, 0:D], ACT.Relu if first else ACT.Copy).then_inc(xt_s[k], 1)

                        for k in range(2):
                            load(a, 0, k)
                        for k in range(2):
                            turned(0, k)
                            load(a, 1, k)
                        with a.Fori(0, PAIRS) as t:
                            for k in range(2):
                                turned(t + 1, k)
                                load(a, t + 2, k)

                        for k in range(2):
                            a.wait_ge(h_in[k], 16 * (PAIRS + 2))

                    @block.gpsimd
                    def _(g):
                        with g.Fori(0, PAIRS + 1) as t:
                            for k in range(2):
                                g.wait_ge(ve_s[k], t + 1)
                                g.tensor_tensor(out=rs[:, k, :], in0=veps[:, k, :], in1=neghalf[:, :],
                                                op=ALU.pow).then_inc(rs_s[k], 1)

                    @block.vector
                    def _(v):
                        if not first:
                            v.wait_ge(w_in_s, 16 * 8)
                            for c in range(2):
                                ins = v.tensor_scalar(out=bmat[:, c, :], in0=ones[:, :], scalar1=bcol[:, c:c + 1],
                                                      scalar2=None, op0=ALU.mult)
                            ins.then_inc(bm, 1)
                            v.wait_ge(bias_mm, 1)
                            v.tensor_tensor(out=bias[:, 0:2 * D], in0=bias[:, 0:2 * D], in1=mma[0][:, 0:2 * D], op=ALU.add)
                            v.tensor_tensor(out=bias[:, 2 * D:W], in0=bias[:, 2 * D:W], in1=mmb[0][:, 0:D],
                                            op=ALU.add).then_inc(wf, 1)
                            for c in range(2):
                                v.tensor_scalar(out=w[:, c, 0:D], in0=w[:, c, 0:D], scalar1=gcol[:, c:c + 1],
                                                scalar2=SCALE, op0=ALU.mult, op1=ALU.mult)
                                ins = v.tensor_scalar(out=w[:, c, D:W], in0=w[:, c, D:W], scalar1=gcol[:, c:c + 1],
                                                      scalar2=None, op0=ALU.mult)
                            ins.then_inc(wf, 1)
                            v.wait_ge(wf, 1)
                            v.tensor_scalar(out=bias[:, 0:D], in0=bias[:, 0:D], scalar1=SCALE, scalar2=None,
                                            op0=ALU.mult).then_inc(bias_ok, 1)
                        else:
                            v.wait_ge(w_in_s, 32)

                        def stats(t, k):
                            v.wait_ge(h_in[k], t * 16 + 16)
                            v.bn_stats(out=st[:, k, :], in_=hin[:, k, :]).then_inc(st_s[k], 1)
                            v.wait_ge(st_s[k], t + 1)
                            v.sem_inc(aggr_go, 1)
                            v.bn_aggr(out=mv[:, k, :], in_=st[:, k, :]).then_inc(mv_s[k], 1)
                            v.wait_ge(mv_s[k], t + 1)
                            v.tensor_scalar(out=veps[:, k, :], in0=mv[:, k, 1:2], scalar1=EPS, scalar2=None,
                                            op0=ALU.add).then_inc(ve_s[k], 1)

                        def norm(t, k):
                            v.wait_ge(rs_s[k], t + 1)
                            v.wait_ge(tr_s[k], t)
                            v.tensor_scalar(out=xn[:, k, :], in0=hin[:, k, :], scalar1=mv[:, k, 0:1],
                                            scalar2=rs[:, k, :], op0=ALU.subtract, op1=ALU.mult).then_inc(xn_s[k], 1)

                        def results(t, k):
                            v.wait_ge(mm_s[k], t + 1)
                            v.wait_ge(kv_out[k], t * (16 if first else 32))
                            if first:
                                v.tensor_tensor(out=res[:, k, :], in0=mma[k][:, 0:D], in1=bias[:, :],
                                                op=ALU.add).then_inc(ev_s[k], 1)
                                return
                            v.tensor_tensor(out=res[:, k, 0:2 * D], in0=mma[k][:, 0:2 * D], in1=bias[:, 0:2 * D], op=ALU.add)
                            v.tensor_tensor(out=res[:, k, 2 * D:W], in0=mmb[k][:, 0:D], in1=bias[:, 2 * D:W],
                                            op=ALU.add).then_inc(ev_s[k], 1)
                            v.wait_ge(ev_s[k], t + 1)
                            v.wait_ge(rd_s[k], t)
                            at = (t * 2 + k) * QW
                            v.tensor_tensor(out=qk[:, k, :], in0=res[:, k, 0:D], in1=res[:, k, D:2 * D],
                                            op=ALU.mult).then_inc(pr_s[k], 1)
                            v.tensor_copy(region[:, bass.ds(at, D)], res[:, k, 0:D])
                            v.wait_ge(pr_s[k], t + 1)
                            v.tensor_reduce(out=region[:, bass.ds(at + D, H)],
                                            in_=qk[:, k, :].rearrange("p (h d) -> p h d", d=DH),
                                            axis=AX.X, op=ALU.add).then_inc(rd_s[k], 1)

                        for k in range(2):
                            stats(0, k)
                        for k in range(2):
                            norm(0, k)
                        with v.Fori(0, PAIRS) as t:
                            for k in range(2):
                                stats(t + 1, k)
                            results(t, 0)
                            for k in range(2):
                                norm(t + 1, k)
                            results(t, 1)

                    @block.tensor
                    def _(pe):
                        if not first:
                            pe.wait_ge(bm, 1)
                            for c in range(2):
                                pe.matmul(mma[0][:, 0:2 * D], bmat[:, c, :], w[:, c, 0:2 * D], start=(c == 0), stop=(c == 1))
                            for c in range(2):
                                ins = pe.matmul(mmb[0][:, 0:D], bmat[:, c, :], w[:, c, 2 * D:W], start=(c == 0), stop=(c == 1))
                            ins.then_inc(bias_mm, 1)
                            pe.wait_ge(wf, 2)
                        else:
                            pe.wait_ge(w_in_s, 32)

                        def turn(t, k):
                            pe.wait_ge(xn_s[k], t + 1)
                            pe.wait_ge(xt_s[k], t)
                            for c in range(2):
                                ins = pe.transpose(tp[k][:, c * P:(c + 1) * P], xn[:, k, c * P:(c + 1) * P], ident[:, :])
                            ins.then_inc(tr_s[k], 1)

                        def products(t, k):
                            pe.wait_ge(xt_s[k], t + 1)
                            pe.wait_ge(ev_s[k], t)
                            for c in range(2):
                                ins = pe.matmul(mma[k][:, 0:min(W, 2 * D)], xT[:, k, c * P:(c + 1) * P],
                                                w[:, c, 0:min(W, 2 * D)], start=(c == 0), stop=(c == 1))
                            if not first:
                                for c in range(2):
                                    ins = pe.matmul(mmb[k][:, 0:D], xT[:, k, c * P:(c + 1) * P],
                                                    w[:, c, 2 * D:W], start=(c == 0), stop=(c == 1))
                            ins.then_inc(mm_s[k], 1)

                        for k in range(2):
                            turn(0, k)
                        with pe.Fori(0, PAIRS) as t:
                            products(t, 0)
                            turn(t + 1, 0)
                            products(t, 1)
                            turn(t + 1, 1)
                end_phase()
        def node_tiles(engine, t):
            return nc.values_load_multi_w_load_instructions(
                nt_row[0:1, bass.ds(t * GI, GI)], engines=[engine], min_val=0, max_val=NT - 1,
                skip_runtime_bounds_check_because="the table is clamped to NT - 1 and counts from 0")[1]

        def edge_scores(S, done):
            with ExitStack() as ph:
                kring = sb(ph, "kring", [P, GI, D])
                idx = sb(ph, "idx", [P, 4, QT], i32)
                drow = sb(ph, "drow", [P, 2, HALF * P])
                hot = sb(ph, "hot", [P, 4, P])
                prod = sb(ph, "prod", [P, 4, D])
                qe = [pb(ph, f"qe{j}") for j in range(4)]
                s = Names(pool)
                drow_s, hoth_s, red_s = (s.many(2) for _ in range(3))
                k_in = ring_in
                hot_s, mm_s, prod_s, idx_s = (s.many(4) for _ in range(4))
                pool_go = s.one()

                with nc.Block() as block:
                    @block.sync
                    def _(sp):
                        with sp.Fori(0, TURNS + 1) as t:
                            for f in range(2):
                                sp.wait_ge(hoth_s[f], t * HALF)
                                sp.dma_start(drow[:, f, :],
                                             drel_d[bass.ds((t * GI + f * HALF) * P, HALF * P)]
                                             .rearrange("(a n) -> a n", a=1).to_broadcast([P, HALF * P])).then_inc(drow_s[f], 16)
                        for f in range(2):
                            sp.wait_ge(drow_s[f], 16 * (TURNS + 1))

                    @block.gpsimd
                    def _(g):
                        with g.Fori(0, TURNS) as t:
                            for q in range(4):
                                g.wait_ge(idx_s[q], t + 1)
                                g.sem_inc(pool_go, 1)
                                for k in range(q * QT, (q + 1) * QT):
                                    g.indirect_dma_start(
                                        out=kring[:, k, :], out_offset=None, in_=Kd,
                                        in_offset=bass.IndirectOffsetOnAxis(ap=idx[:, q, k % QT:k % QT + 1], axis=0)
                                    ).then_inc(k_in[k], 16)
                        for k in range(GI):
                            g.wait_ge(k_in[k], done + 16 * TURNS)

                    @block.scalar
                    def _(a):
                        def sources(t, q):
                            a.activation(idx[:, q, :], src_c[:, bass.ds(t * GI + q * QT, QT)], ACT.Copy).then_inc(idx_s[q], 1)

                        for q in range(4):
                            sources(0, q)
                        with a.Fori(0, TURNS) as t:
                            for f in range(2):
                                for q in (2 * f, 2 * f + 1):
                                    a.wait_ge(red_s[f], t * HALF + (q % 2 + 1) * QT)
                                    sources(t + 1, q)
                    @block.vector
                    def _(v):
                        def one_hot(t, k):
                            f, j, use = k // HALF, k % 4, k // 4
                            if k % HALF == 0:
                                v.wait_ge(drow_s[f], t * 16 + 16)
                            v.wait_ge(mm_s[j], t * 4 + use)
                            v.tensor_scalar(out=hot[:, j, :], in0=drow[:, f, (k % HALF) * P:(k % HALF + 1) * P],
                                            scalar1=iota_p[:, :], scalar2=None, op0=ALU.is_equal
                                            ).then_inc(hot_s[j], 1)

                        def reduce(t, k):
                            f, j, use = k // HALF, k % 4, k // 4
                            v.wait_ge(prod_s[j], t * 4 + use + 1)
                            v.tensor_reduce(out=S[:, 0:H, bass.ds(t * GI + k, 1)],
                                            in_=prod[:, j, :].rearrange("p (h d) -> p h d", d=DH),
                                            axis=AX.X, op=ALU.add).then_inc(red_s[f], 1)

                        for k in range(3):
                            one_hot(0, k)
                        with v.Fori(0, TURNS) as t:
                            for k in range(GI):
                                f, j, use = k // HALF, k % 4, k // 4
                                v.wait_ge(mm_s[j], t * 4 + use + 1)
                                v.tensor_copy(S[:, H:2 * H, bass.ds(t * GI + k, 1)], qe[j][:, D:QW].unsqueeze(2))
                                v.wait_ge(k_in[k], t * 16 + done + 16)
                                if k % HALF >= 4:
                                    v.wait_ge(red_s[f], t * HALF + k % HALF - 3)
                                elif k < HALF:
                                    v.wait_ge(red_s[1], t * HALF)
                                else:
                                    v.wait_ge(red_s[0], t * HALF + HALF - 4 + k % HALF + 1)
                                v.tensor_tensor(out=prod[:, j, :], in0=qe[j][:, 0:D], in1=kring[:, k, :],
                                                op=ALU.mult).then_inc(prod_s[j], 1)
                                if k + 3 >= GI:
                                    one_hot(t + 1, k + 3 - GI)
                                else:
                                    one_hot(t, k + 3)
                                    if (k + 3) % HALF == HALF - 1:
                                        half_read = (k + 3) // HALF
                                        v.wait_ge(hot_s[(k + 3) % 4], t * 4 + (k + 3) // 4 + 1)
                                        v.sem_inc(hoth_s[half_read], HALF)
                                reduce(t, k)

                    @block.tensor
                    def _(pe):
                        with pe.Fori(0, TURNS) as t:
                            ns = node_tiles(mybir.EngineType.PE, t)
                            for k in range(GI):
                                n, j, use = ns[k], k % 4, k // 4
                                pe.wait_ge(hot_s[j], t * 4 + use + 1)
                                pe.wait_ge(prod_s[j], t * 4 + use)
                                pe.matmul(qe[j][:, 0:QW], hot[:, j, :], region[:, bass.ds(n * QW, QW)],
                                          start=True, stop=True).then_inc(mm_s[j], 1)
                end_phase()

        def edge_weights(S):
            flat = S[:, :, :].rearrange("p r i -> p (r i)")
            sc, own, mx = region[:, 0:SL], region[:, SL:2 * SL], region[:, 2 * SL:3 * SL]
            QB = IG // 4
            with ExitStack() as ph:
                stage = sb(ph, "stage", [P, 2, 4, P])
                diff = sb(ph, "diff", [P, 2, 512])
                ex = sb(ph, "ex", [P, 2, 512])
                end_row = sb(ph, "end_row", [1, P])
                carry = sb(ph, "carry", [1, P + 1])
                take = sb(ph, "take", [1, P])
                init = sb(ph, "init", [P, 1])
                psc, pown = pb(ph, "psc"), pb(ph, "pown")
                small = pb(ph, "small")
                s = Names(pool)
                st_a, st_v, tr_a, tr_v, out_a, out_v = s.many(6)
                with nc.Block() as block:
                    @block.scalar
                    def _(a):
                        with a.Fori(0, QB) as t:
                            a.wait_ge(tr_a, t)
                            for b in range(4):
                                ins = a.activation(stage[:, 0, b, :],
                                                   flat[:, bass.ds(t * 4 + b, P, step=IG)], ACT.Copy)
                            ins.then_inc(st_a, 1)
                            a.wait_ge(tr_a, t + 1)
                            a.activation(sc[:, bass.ds(t * 512, 512)], psc[:, :], ACT.Copy).then_inc(out_a, 1)

                    @block.vector
                    def _(v):
                        with v.Fori(0, QB) as t:
                            v.wait_ge(tr_v, t)
                            for b in range(4):
                                ins = v.tensor_copy(stage[:, 1, b, :],
                                                    flat[:, bass.ds(H * NI + t * 4 + b, P, step=IG)])
                            ins.then_inc(st_v, 1)
                            v.wait_ge(tr_v, t + 1)
                            v.tensor_copy(own[:, bass.ds(t * 512, 512)], pown[:, :]).then_inc(out_v, 1)

                    @block.tensor
                    def _(pe):
                        with pe.Fori(0, QB) as t:
                            for which, staged, out_s, done, bank in ((0, st_a, out_a, tr_a, psc), (1, st_v, out_v, tr_v, pown)):
                                pe.wait_ge(staged, t + 1)
                                pe.wait_ge(out_s, t)
                                for b in range(4):
                                    ins = pe.transpose(bank[:, b * P:(b + 1) * P], stage[:, which, b, :], ident[:, :])
                                ins.then_inc(done, 1)
                end_phase()

                s = Names(pool)
                c, rowed, back = s.many(3)
                with nc.Block() as block:
                    @block.vector
                    def _(v):
                        v.tensor_tensor(out=mx, in0=sc, in1=own, op=ALU.max).then_inc(c, 1)
                        for way in range(2):
                            run = (lambda z: z) if way == 0 else (lambda z: z[:, ::-1])
                            reset = run((reset_f, reset_b)[way][:, :])
                            chain = run((chain_f, chain_b)[way][0:1, :])
                            i = 7 * way
                            v.wait_ge(c, i + 1)
                            v.tensor_tensor_scan(run(mx), reset, run(mx), -BIG, ALU.add, ALU.max).then_inc(c, 1)
                            v.wait_ge(rowed, way + 1)
                            v.tensor_copy(end_row[:, :], small[0:1, 0:P]).then_inc(c, 1)
                            v.wait_ge(c, i + 3)
                            v.tensor_tensor_scan(run(carry[0:1, 0:P]), chain, run(end_row[0:1, :]), -BIG,
                                                 ALU.add, ALU.max).then_inc(c, 1)
                            v.wait_ge(c, i + 4)
                            if way == 0:
                                v.tensor_copy(take[0:1, 1:P], carry[0:1, 0:P - 1]).then_inc(c, 1)
                                v.wait_ge(c, i + 5)
                                v.memset(take[0:1, 0:P:CH], -BIG).then_inc(c, 1)
                            else:
                                v.tensor_copy(take[0:1, 0:P - 1], carry[0:1, 1:P]).then_inc(c, 1)
                                v.wait_ge(c, i + 5)
                                v.memset(take[0:1, CH - 1:P:CH], -BIG).then_inc(c, 1)
                            v.wait_ge(back, way + 1)
                            v.tensor_copy(init[:, :], small[:, P:P + 1]).then_inc(c, 1)
                            v.wait_ge(c, i + 7)
                            v.tensor_tensor_scan(run(mx), reset, run(mx), init[:, 0:1], ALU.add, ALU.max).then_inc(c, 1)

                    @block.tensor
                    def _(pe):
                        for way in range(2):
                            pe.wait_ge(c, 7 * way + 2)
                            last = mx[:, SL - 1:SL] if way == 0 else mx[:, 0:1]
                            pe.transpose(small[0:1, 0:P], last, ident[:, :]).then_inc(rowed, 1)
                            pe.wait_ge(c, 7 * way + 6)
                            pe.matmul(small[:, P:P + 1], take[0:1, :], ones[0:1, 0:1], start=True, stop=True).then_inc(back, 1)
                end_phase()

                s = Names(pool)
                df, ew, mw, tr, out_a, out_v = s.many(6)
                dg, eo, tro = s.many(3)
                with nc.Block() as block:
                    @block.gpsimd
                    def _(g):
                        with g.Fori(0, QB) as t:
                            g.wait_ge(eo, t)
                            g.tensor_tensor(out=diff[:, 1, :], in0=own[:, bass.ds(t * 512, 512)],
                                            in1=mx[:, bass.ds(t * 512, 512)], op=ALU.subtract).then_inc(dg, 1)

                    @block.vector
                    def _(v):
                        with v.Fori(0, QB) as t:
                            v.wait_ge(ew, t)
                            v.tensor_tensor(out=diff[:, 0, :], in0=sc[:, bass.ds(t * 512, 512)],
                                            in1=mx[:, bass.ds(t * 512, 512)], op=ALU.subtract).then_inc(df, 1)
                            v.wait_ge(eo, t + 1)
                            v.wait_ge(tro, t)
                            v.scalar_tensor_tensor(out=stage[:, 1, :, :].rearrange("p b e -> p (b e)"),
                                                   in0=reset_f[:, bass.ds(t * 512, 512)],
                                                   scalar=-1.0 / BIG, in1=ex[:, 1, :], op0=ALU.mult,
                                                   op1=ALU.mult).then_inc(mw, 1)
                            v.wait_ge(tro, t + 1)
                            v.tensor_copy(flat[:, H * NI:2 * H * NI].rearrange("p (q g) -> p q g", g=IG)[:, :, bass.ds(t * 4, 4)],
                                          pown[:, :].rearrange("p (b q) -> p q b", b=4)).then_inc(out_v, 1)

                    @block.scalar
                    def _(a):
                        with a.Fori(0, QB) as t:
                            a.wait_ge(df, t + 1)
                            a.wait_ge(tr, t)
                            a.activation(stage[:, 0, :, :].rearrange("p b e -> p (b e)"), diff[:, 0, :], ACT.Exp).then_inc(ew, 1)
                            a.wait_ge(dg, t + 1)
                            a.wait_ge(mw, t)
                            a.activation(ex[:, 1, :], diff[:, 1, :], ACT.Exp).then_inc(eo, 1)
                            a.wait_ge(tr, t + 1)
                            a.activation(flat[:, 0:H * NI].rearrange("p (q g) -> p q g", g=IG)[:, :, bass.ds(t * 4, 4)],
                                         psc[:, :].rearrange("p (b q) -> p q b", b=4), ACT.Copy).then_inc(out_a, 1)

                    @block.tensor
                    def _(pe):
                        with pe.Fori(0, QB) as t:
                            for which, made, out_s, done, bank in ((0, ew, out_a, tr, psc), (1, mw, out_v, tro, pown)):
                                pe.wait_ge(made, t + 1)
                                pe.wait_ge(out_s, t)
                                for b in range(4):
                                    ins = pe.transpose(bank[:, b * P:(b + 1) * P], stage[:, which, b, :], ident[:, :])
                                ins.then_inc(done, 1)
                end_phase()

        def edge_sums(S, done):
            with ExitStack() as ph:
                vring = sb(ph, "vring", [P, GI, D])
                idx = sb(ph, "idx", [P, 4, QT], i32)
                hot = sb(ph, "hot", [P, 4, P])
                msg = sb(ph, "msg", [P, 4, XW])
                sums = [pb(ph, f"sums{j}") for j in range(4)]
                s = Names(pool)
                v_in = ring_in
                msg_s, w_s, mm_s, acc_s, idx_s = (s.many(4) for _ in range(5))
                pool_go, zeroed = s.many(2)

                with nc.Block() as block:
                    @block.gpsimd
                    def _(g):
                        with g.Fori(0, TURNS) as t:
                            for q in range(4):
                                g.wait_ge(idx_s[q], t + 1)
                                g.sem_inc(pool_go, 1)
                                for k in range(q * QT, (q + 1) * QT):
                                    g.indirect_dma_start(
                                        out=vring[:, k, :], out_offset=None, in_=Vd,
                                        in_offset=bass.IndirectOffsetOnAxis(ap=idx[:, q, k % QT:k % QT + 1], axis=0)
                                    ).then_inc(v_in[k], 16)
                        for k in range(GI):
                            g.wait_ge(v_in[k], done + 16 * TURNS)

                    @block.scalar
                    def _(a):
                        def sources(t, q):
                            a.activation(idx[:, q, :], src_c[:, bass.ds(t * GI + q * QT, QT)], ACT.Copy).then_inc(idx_s[q], 1)

                        for q in range(4):
                            sources(0, q)
                        a.wait_ge(zeroed, 1)
                        with a.Fori(0, TURNS) as t:
                            for q in range(4):
                                for j in range(4):
                                    a.wait_ge(mm_s[j], t * 4 + q)
                                    a.activation(msg[:, j, D:D + 2 * H].unsqueeze(2),
                                                 S[:, :, bass.ds(t * GI + q * QT + j, 1)], ACT.Copy).then_inc(w_s[j], 1)
                                a.wait_ge(msg_s[3], t * 4 + q + 1)
                                sources(t + 1, q)

                    @block.vector
                    def _(v):
                        v.memset(region[:, 0:(NT + 2) * XW], 0.0)
                        for j in range(4):
                            ins = v.memset(msg[:, j, D + 2 * H:XW], 1.0)
                        ins.then_inc(zeroed, 1)
                        v.wait_ge(zeroed, 1)

                        def add(t, k, n):
                            j, use = k % 4, k // 4
                            v.wait_ge(mm_s[j], t * 4 + use + 1)
                            if k:
                                v.wait_ge(acc_s[(k - 1) % 4], t * 4 + (k - 1) // 4 + 1)
                            else:
                                v.wait_ge(acc_s[3], t * 4)
                            v.tensor_tensor(out=region[:, bass.ds(n * XW, XW)], in0=region[:, bass.ds(n * XW, XW)],
                                            in1=sums[j][:, 0:XW], op=ALU.add).then_inc(acc_s[j], 1)

                        with v.Fori(0, TURNS) as t:
                            ns = node_tiles(mybir.EngineType.DVE, t)
                            for k in range(GI):
                                j, use = k % 4, k // 4
                                v.wait_ge(mm_s[j], t * 4 + use)
                                v.tensor_scalar(out=hot[:, j, :], in0=iota_f[:, :],
                                                scalar1=drel_c[:, bass.ds(t * GI + k, 1)], scalar2=None,
                                                op0=ALU.is_equal)
                                v.wait_ge(v_in[k], t * 16 + done + 16)
                                v.tensor_tensor(out=msg[:, j, 0:D].rearrange("p (h d) -> p h d", d=DH),
                                                in0=vring[:, k, :].rearrange("p (h d) -> p h d", d=DH),
                                                in1=S[:, 0:H, bass.ds(t * GI + k, 1)].to_broadcast([P, H, DH]),
                                                op=ALU.mult).then_inc(msg_s[j], 1)
                                if k >= 2:
                                    add(t, k - 2, ns[k - 2])
                            add(t, GI - 2, ns[GI - 2])
                            add(t, GI - 1, ns[GI - 1])

                    @block.tensor
                    def _(pe):
                        with pe.Fori(0, TURNS) as t:
                            for k in range(GI):
                                j, use = k % 4, k // 4
                                pe.wait_ge(msg_s[j], t * 4 + use + 1)
                                pe.wait_ge(w_s[j], t * 4 + use + 1)
                                pe.wait_ge(acc_s[j], t * 4 + use)
                                pe.matmul(sums[j][:, 0:XW], hot[:, j, :], msg[:, j, :],
                                          start=True, stop=True).then_inc(mm_s[j], 1)
                end_phase()
        def update(l):
            FB = FF // P
            with ExitStack() as ph:
                wo_s = sb(ph, "wo_s", [P, 2, D])
                w1_s = sb(ph, "w1_s", [P, 2, FF])
                w2_s = sb(ph, "w2_s", [P, FB, D])
                bo_b = sb(ph, "bo_b", [P, D])
                b2_b = sb(ph, "b2_b", [P, D])
                b1_c = sb(ph, "b1_c", [P, FB])
                gcol = sb(ph, "gcol", [P, 2])
                bcol = sb(ph, "bcol", [P, 2])
                hin = sb(ph, "hin", [P, 2, D])
                vin = sb(ph, "vin", [P, 2, D])
                hb = sb(ph, "hb", [P, 2, D])
                h1 = sb(ph, "h1", [P, 2, D])
                h1b = sb(ph, "h1b", [P, 2, D])
                res = sb(ph, "res", [P, 2, D])
                zt = sb(ph, "zt", [P, 2, 3, H])
                own = sb(ph, "own", [P, 2, D])
                agg = sb(ph, "agg", [P, 2, D])
                att = sb(ph, "att", [P, 2, D])
                st = sb(ph, "st", [P, 2, 6])
                mv = sb(ph, "mv", [P, 2, 2])
                veps = sb(ph, "veps", [P, 2, 1])
                rs = sb(ph, "rs", [P, 2, 1])
                xn = sb(ph, "xn", [P, 2, D])
                aT = sb(ph, "aT", [P, 2, D])
                xT = sb(ph, "xT", [P, 2, D])
                uT = sb(ph, "uT", [P, 2, FB, P])
                ea = sb(ph, "ea", [P, 2, EG, YW])
                srow = sb(ph, "srow", [P, 2, EG * P], i32)
                scol = sb(ph, "scol", [P, 2, EG], i32)
                scol_f = sb(ph, "scol_f", [P, 2, EG])
                same = sb(ph, "same", [P, 2, EG, P])
                before = sb(ph, "before", [P, EG, P])
                count = sb(ph, "count", [P, 2, EG])
                away = sb(ph, "away", [P, 2, 2, EG])
                dest = sb(ph, "dest", [P, 2, EG], i32)
                dummy = sb(ph, "dummy", [P, 1])
                ysum = sb(ph, "ysum", [P, 2, EG, YW])
                tp = [pb(ph, f"tp{k}") for k in range(2)]
                wo_p, w2_p = pb(ph, "wo_p"), pb(ph, "w2_p")
                w1_p = [pb(ph, f"w1_p{f}") for f in range(2)]
                y_p = [pb(ph, f"y_p{b}") for b in range(2)]
                PARTS = ((0, 0, 3), (1, 3, 6), (0, 6, EG))
                s = Names(pool)
                w_in_s, prep, bmm, const_s, pool_go, join, s3_c, aggr_go = s.many(8)
                hv_in, e_in, n_c, hb_s, ta_s, at_s, wo_d, h1_s, st_s, mv_s, ve_s, rs_s = (s.many(2) for _ in range(12))
                h1b_s, xn_s, tx_s, xt_s, w1_d, gel, w2_d, out_s, stored, y_d, y_ev, idx_s = (s.many(2) for _ in range(12))
                sc0 = l * 32 * PAIRS
                S3N = EG + 5

                with nc.Block() as block:
                    @block.sync
                    def _(sp):
                        slow = dict(allow_slow_non_contiguous=True)
                        sp.dma_start(wo_s[:, :, :], wo[l].rearrange("(c p) n -> p c n", p=P)).then_inc(w_in_s, 16)
                        sp.dma_start(w1_s[:, :, :], w1[l].rearrange("(c p) n -> p c n", p=P)).then_inc(w_in_s, 16)
                        sp.dma_start(w2_s[:, :, :], w2[l].rearrange("(c p) n -> p c n", p=P)).then_inc(w_in_s, 16)
                        sp.dma_start(bo_b[:, :], bo[l:l + 1, :].to_broadcast([P, D])).then_inc(w_in_s, 16)
                        sp.dma_start(b2_b[:, :], b2[l:l + 1, :].to_broadcast([P, D])).then_inc(w_in_s, 16)
                        sp.dma_start(b1_c[:, :], b1[l].rearrange("(c p) -> p c", p=P), **slow).then_inc(w_in_s, 16)
                        sp.dma_start(gcol[:, :], ln2_g[l].rearrange("(c p) -> p c", p=P), **slow).then_inc(w_in_s, 16)
                        sp.dma_start(bcol[:, :], ln2_b[l].rearrange("(c p) -> p c", p=P), **slow).then_inc(w_in_s, 16)
                        sp.wait_ge(const_s, 1)

                        def load_nodes(t, k):
                            sp.dma_start(hin[:, k, :], rows(Hd, t * 2 + k)).then_inc(hv_in[k], 16)
                            sp.dma_start(vin[:, k, :], rows(Vd, t * 2 + k)).then_inc(hv_in[k], 16)

                        def load_edges(t, k):
                            g = l * NT + t * 2 + k
                            sp.dma_start(ea[:, k, :, 0:ED],
                                         edge_attr[bass.ds(g * P, P), :].rearrange("p (j w) -> p j w", w=ED)).then_inc(e_in[k], 16)
                            sp.dma_start(srow[:, k, :], src_rows[bass.ds(g, 1), :].to_broadcast([P, EG * P])).then_inc(e_in[k], 16)
                            sp.dma_start(scol[:, k, :], src_cols[bass.ds(g * P, P), :]).then_inc(e_in[k], 16)

                        for k in range(2):
                            load_nodes(0, k)
                            load_edges(0, k)
                        for k in range(2):
                            sp.wait_ge(hb_s[k], 1)
                            sp.wait_ge(n_c[k], 6)
                            load_nodes(1, k)
                        with sp.Fori(0, PAIRS) as t:
                            for k in range(2):
                                sp.wait_ge(hb_s[k], t + 2)
                                sp.wait_ge(n_c[k], t * 6 + 12)
                                load_nodes(t + 2, k)
                            for k in range(2):
                                sp.wait_ge(out_s[k], t + 1)
                                sp.dma_start(rows(Hd, t * 2 + k), res[:, k, :]).then_inc(stored[k], 16)
                                sp.wait_ge(y_ev[0], t * 4 + k * 2 + 2)
                                load_edges(t + 1, k)
                        for k in range(2):
                            sp.wait_ge(stored[k], 16 * PAIRS)
                            sp.wait_ge(hv_in[k], 32 * (PAIRS + 2))
                            sp.wait_ge(e_in[k], 48 * (PAIRS + 1))

                    @block.gpsimd
                    def _(g):
                        g.wait_ge(w_in_s, 16 * 8)

                        def add_bo(t, k):
                            g.wait_ge(hv_in[k], t * 32 + 32)
                            g.wait_ge(h1_s[k], t)
                            g.tensor_tensor(out=hb[:, k, :], in0=hin[:, k, :], in1=bo_b[:, :], op=ALU.add).then_inc(hb_s[k], 1)

                        def scale(t, k):
                            g.wait_ge(ve_s[k], t + 1)
                            g.tensor_tensor(out=rs[:, k, :], in0=veps[:, k, :], in1=neghalf[:, :], op=ALU.pow).then_inc(rs_s[k], 1)
                            g.wait_ge(out_s[k], t)
                            g.tensor_tensor(out=h1b[:, k, :], in0=h1[:, k, :], in1=b2_b[:, :], op=ALU.add).then_inc(h1b_s[k], 1)

                        def scatter(t, k):
                            g.wait_ge(idx_s[k], t + 1)
                            for b, j0, j1 in PARTS:
                                if b == 0:
                                    g.wait_ge(y_ev[0], t * 4 + k * 2 + (1 if j0 == 0 else 2))
                                else:
                                    g.wait_ge(y_ev[1], t * 2 + k + 1)
                                for j in range(j0, j1):
                                    r = j % TABLES
                                    if j >= TABLES:
                                        g.wait_ge(sc_s[k][r], t * 32 + sc0 + 16)
                                    elif k == 0:
                                        g.wait_ge(sc_s[1][r], t * 32 + sc0)
                                    else:
                                        g.wait_ge(sc_s[0][r], t * 32 + sc0 + 32)
                                    g.sem_inc(pool_go, 1)
                                    g.indirect_dma_start(
                                        out=sum_d[r], out_offset=bass.IndirectOffsetOnAxis(ap=dest[:, k, j:j + 1], axis=0),
                                        in_=ysum[:, k, j, :], in_offset=None, compute_op=ALU.add).then_inc(sc_s[k][r], 16)

                        for k in range(2):
                            add_bo(0, k)
                        for k in range(2):
                            scale(0, k)
                        with g.Fori(0, PAIRS) as t:
                            for k in range(2):
                                add_bo(t + 1, k)
                            for k in range(2):
                                scale(t + 1, k)
                                scatter(t, k)
                        for k in range(2):
                            for r in range(TABLES):
                                g.wait_ge(sc_s[k][r], sc0 + 32 * PAIRS)

                    @block.vector
                    def _(v):
                        for k in range(2):
                            ins = v.memset(ea[:, k, :, ED:YW], 1.0)
                        ins.then_inc(const_s, 1)
                        v.tensor_scalar(out=dummy[:, :], in0=iota_p[:, :], scalar1=float(DUMMY), scalar2=None,
                                        op0=ALU.add).then_inc(join, 1)
                        v.wait_ge(w_in_s, 16 * 8)
                        v.wait_ge(bmm, 1)
                        v.tensor_tensor(out=b1_c[:, :], in0=b1_c[:, :], in1=w2_p[:, 0:FB], op=ALU.add)
                        for c in range(2):
                            ins = v.tensor_scalar(out=w1_s[:, c, :], in0=w1_s[:, c, :], scalar1=gcol[:, c:c + 1],
                                                  scalar2=None, op0=ALU.mult)
                        ins.then_inc(prep, 1)
                        v.wait_ge(join, 1)

                        def heads(ap):
                            return ap.rearrange("p (h d) -> p h d", d=DH)

                        def attention(t, k):
                            at = (t * 2 + k) * XW
                            v.wait_ge(ta_s[k], t)
                            v.tensor_tensor(out=zt[:, k, 0, :], in0=region[:, bass.ds(at + D, H)],
                                            in1=region[:, bass.ds(at + D + H, H)], op=ALU.add).then_inc(n_c[k], 1)
                            v.wait_ge(hv_in[k], t * 32 + 32)
                            v.tensor_tensor(out=heads(own[:, k, :]), in0=heads(vin[:, k, :]),
                                            in1=region[:, bass.ds(at + D + H, H)].unsqueeze(2).to_broadcast([P, H, DH]),
                                            op=ALU.mult).then_inc(n_c[k], 1)
                            v.wait_ge(n_c[k], t * 6 + 1)
                            v.scalar_tensor_tensor(out=zt[:, k, 1, :], in0=zt[:, k, 0, :], scalar=0.0, in1=zt[:, k, 0, :],
                                                   op0=ALU.is_equal, op1=ALU.add).then_inc(n_c[k], 1)
                            v.wait_ge(n_c[k], t * 6 + 2)
                            v.tensor_tensor(out=agg[:, k, :], in0=own[:, k, :], in1=region[:, bass.ds(at, D)],
                                            op=ALU.add).then_inc(n_c[k], 1)
                            v.wait_ge(n_c[k], t * 6 + 3)
                            v.reciprocal(zt[:, k, 2, :], zt[:, k, 1, :]).then_inc(n_c[k], 1)
                            v.wait_ge(n_c[k], t * 6 + 5)
                            v.tensor_tensor(out=heads(att[:, k, :]), in0=heads(agg[:, k, :]),
                                            in1=zt[:, k, 2, :].unsqueeze(2).to_broadcast([P, H, DH]),
                                            op=ALU.mult).then_inc(n_c[k], 1)

                        def stats(t, k):
                            v.wait_ge(wo_d[k], t + 1)
                            v.wait_ge(hb_s[k], t + 1)
                            v.wait_ge(h1b_s[k], t)
                            v.tensor_tensor(out=h1[:, k, :], in0=wo_p[:, k * D:(k + 1) * D], in1=hb[:, k, :],
                                            op=ALU.add).then_inc(h1_s[k], 1)
                            v.wait_ge(h1_s[k], t + 1)
                            v.bn_stats(out=st[:, k, :], in_=h1[:, k, :]).then_inc(st_s[k], 1)
                            v.wait_ge(st_s[k], t + 1)
                            v.sem_inc(aggr_go, 1)
                            v.bn_aggr(out=mv[:, k, :], in_=st[:, k, :]).then_inc(mv_s[k], 1)
                            v.wait_ge(mv_s[k], t + 1)
                            v.tensor_scalar(out=veps[:, k, :], in0=mv[:, k, 1:2], scalar1=EPS, scalar2=None,
                                            op0=ALU.add).then_inc(ve_s[k], 1)

                        def norm(t, k):
                            v.wait_ge(rs_s[k], t + 1)
                            v.wait_ge(tx_s[k], t)
                            v.tensor_scalar(out=xn[:, k, :], in0=h1[:, k, :], scalar1=mv[:, k, 0:1],
                                            scalar2=rs[:, k, :], op0=ALU.subtract, op1=ALU.mult).then_inc(xn_s[k], 1)

                        def result(t, k):
                            v.wait_ge(w2_d[k], t + 1)
                            v.wait_ge(h1b_s[k], t + 1)
                            v.wait_ge(stored[k], t * 16)
                            v.tensor_tensor(out=res[:, k, :], in0=w2_p[:, k * D:(k + 1) * D], in1=h1b[:, k, :],
                                            op=ALU.add).then_inc(out_s[k], 1)

                        def repeats(t, k):
                            at = (t * 2 + k) * S3N
                            v.wait_ge(e_in[k], t * 48 + 48)
                            v.tensor_copy(scol_f[:, k, :], scol[:, k, :]).then_inc(s3_c, 1)
                            v.wait_ge(s3_c, at + 1)
                            for j in range(EG):
                                ins = v.tensor_scalar(out=same[:, k, j, :], in0=srow[:, k, j * P:(j + 1) * P],
                                                      scalar1=scol_f[:, k, j:j + 1], scalar2=None, op0=ALU.is_equal)
                            ins.then_inc(s3_c, 1)
                            v.wait_ge(s3_c, at + 2)
                            for j in range(EG):
                                v.tensor_tensor_reduce(out=before[:, j, :], in0=same[:, k, j, :], in1=tril[:, :], scale=1.0,
                                                       scalar=0.0, op0=ALU.mult, op1=ALU.add,
                                                       accum_out=count[:, k, j:j + 1]).then_inc(s3_c, 1)
                            v.tensor_scalar(out=away[:, k, 0, :], in0=scol_f[:, k, :], scalar1=-1.0, scalar2=dummy[:, 0:1],
                                            op0=ALU.mult, op1=ALU.add).then_inc(s3_c, 1)
                            v.wait_ge(s3_c, at + EG + 3)
                            v.scalar_tensor_tensor(out=away[:, k, 1, :], in0=count[:, k, :], scalar=0.0, in1=away[:, k, 0, :],
                                                   op0=ALU.is_gt, op1=ALU.mult).then_inc(s3_c, 1)
                            v.wait_ge(s3_c, at + EG + 4)
                            for r in range(TABLES):
                                v.wait_ge(sc_s[k][r], t * 32 + sc0)
                            v.tensor_tensor(out=dest[:, k, :], in0=away[:, k, 1, :], in1=scol_f[:, k, :],
                                            op=ALU.add).then_inc(idx_s[k], 1)
                            v.wait_ge(idx_s[k], t + 1)
                            v.sem_inc(s3_c, 1)

                        for k in range(2):
                            attention(0, k)
                        for k in range(2):
                            stats(0, k)
                        for k in range(2):
                            norm(0, k)
                        with v.Fori(0, PAIRS) as t:
                            attention(t + 1, 0)
                            repeats(t, 0)
                            result(t, 0)
                            stats(t + 1, 0)
                            attention(t + 1, 1)
                            norm(t + 1, 0)
                            repeats(t, 1)
                            result(t, 1)
                            stats(t + 1, 1)
                            norm(t + 1, 1)

                    @block.scalar
                    def _(a):
                        def turned_att(t, k):
                            a.wait_ge(ta_s[k], t + 1)
                            a.wait_ge(wo_d[k], t)
                            a.activation(aT[:, k, :], tp[k][:, 0:D], ACT.Copy).then_inc(at_s[k], 1)

                        def turned_norm(t, k):
                            a.wait_ge(tx_s[k], t + 1)
                            a.wait_ge(w1_d[k], t * 2)
                            a.activation(xT[:, k, :], tp[k][:, D:2 * D], ACT.Copy).then_inc(xt_s[k], 1)

                        def gelu(t, k):
                            a.wait_ge(w2_d[k], t)
                            for f in range(2):
                                a.wait_ge(w1_d[k], t * 2 + f + 1)
                                for b in range(4):
                                    j = f * 4 + b
                                    ins = a.activation(uT[:, k, j, :], w1_p[f][:, b * P:(b + 1) * P], ACT.Gelu,
                                                       bias=b1_c[:, j:j + 1])
                                ins.then_inc(gel[f], 1)

                        def sums_out(t, k):
                            for r in range(TABLES):
                                a.wait_ge(sc_s[k][r], t * 32 + sc0)
                            for b, j0, j1 in PARTS:
                                if b == 0:
                                    a.wait_ge(y_d[0], t * 4 + k * 2 + (1 if j0 == 0 else 2))
                                else:
                                    a.wait_ge(y_d[1], t * 2 + k + 1)
                                a.activation(ysum[:, k, j0:j1, :].rearrange("p j w -> p (j w)"),
                                             y_p[b][:, 0:(j1 - j0) * YW], ACT.Copy).then_inc(y_ev[b], 1)

                        for k in range(2):
                            turned_att(0, k)
                        for k in range(2):
                            turned_norm(0, k)
                        a.wait_ge(prep, 1)
                        with a.Fori(0, PAIRS) as t:
                            gelu(t, 0)
                            turned_att(t + 1, 0)
                            sums_out(t, 0)
                            gelu(t, 1)
                            turned_att(t + 1, 1)
                            turned_norm(t + 1, 0)
                            sums_out(t, 1)
                            turned_norm(t + 1, 1)

                    @block.tensor
                    def _(pe):
                        pe.wait_ge(w_in_s, 16 * 8)
                        for j in range(FB):
                            for c in range(2):
                                ins = pe.matmul(w2_p[:, j:j + 1], w1_s[:, c, j * P:(j + 1) * P], bcol[:, c:c + 1],
                                                start=(c == 0), stop=(c == 1))
                        ins.then_inc(bmm, 1)
                        pe.wait_ge(prep, 1)

                        def turn_att(t, k):
                            pe.wait_ge(n_c[k], t * 6 + 6)
                            pe.wait_ge(xt_s[k], t)
                            for c in range(2):
                                ins = pe.transpose(tp[k][:, c * P:(c + 1) * P], att[:, k, c * P:(c + 1) * P], ident[:, :])
                            ins.then_inc(ta_s[k], 1)

                        def out_proj(t, k):
                            pe.wait_ge(at_s[k], t + 1)
                            pe.wait_ge(h1_s[1 - k], t + k)
                            for c in range(2):
                                ins = pe.matmul(wo_p[:, k * D:(k + 1) * D], aT[:, k, c * P:(c + 1) * P], wo_s[:, c, :],
                                                start=(c == 0), stop=(c == 1))
                            ins.then_inc(wo_d[k], 1)

                        def turn_norm(t, k):
                            pe.wait_ge(xn_s[k], t + 1)
                            pe.wait_ge(at_s[k], t + 1)
                            for c in range(2):
                                ins = pe.transpose(tp[k][:, D + c * P:D + (c + 1) * P], xn[:, k, c * P:(c + 1) * P], ident[:, :])
                            ins.then_inc(tx_s[k], 1)

                        def up(t, k):
                            pe.wait_ge(xt_s[k], t + 1)
                            for f in range(2):
                                pe.wait_ge(gel[f], t * 2 + k)
                                for b in range(4):
                                    j = f * 4 + b
                                    for c in range(2):
                                        ins = pe.matmul(w1_p[f][:, b * P:(b + 1) * P], w1_s[:, c, j * P:(j + 1) * P],
                                                        xT[:, k, c * P:(c + 1) * P], start=(c == 0), stop=(c == 1))
                                ins.then_inc(w1_d[k], 1)

                        def down(t, k):
                            pe.wait_ge(out_s[1 - k], t + k)
                            for f in range(2):
                                pe.wait_ge(gel[f], t * 2 + k + 1)
                                for b in range(4):
                                    j = f * 4 + b
                                    ins = pe.matmul(w2_p[:, k * D:(k + 1) * D], uT[:, k, j, :], w2_s[:, j, :],
                                                    start=(j == 0), stop=(j == FB - 1))
                            ins.then_inc(w2_d[k], 1)

                        def sum_group(t, k):
                            pe.wait_ge(e_in[k], t * 48 + 48)
                            pe.wait_ge(s3_c, (t * 2 + k) * S3N + 2)
                            for b, j0, j1 in PARTS:
                                if b == 0:
                                    pe.wait_ge(y_ev[0], t * 4 + k * 2 + (0 if j0 == 0 else 1))
                                else:
                                    pe.wait_ge(y_ev[1], t * 2 + k)
                                for j in range(j0, j1):
                                    ins = pe.matmul(y_p[b][:, (j - j0) * YW:(j - j0 + 1) * YW], same[:, k, j, :],
                                                    ea[:, k, j, :], start=True, stop=True)
                                ins.then_inc(y_d[b], 1)

                        for k in range(2):
                            turn_att(0, k)
                        for k in range(2):
                            out_proj(0, k)
                        for k in range(2):
                            turn_norm(0, k)
                        with pe.Fori(0, PAIRS) as t:
                            up(t, 0)
                            turn_att(t + 1, 0)
                            down(t, 0)
                            out_proj(t + 1, 0)
                            sum_group(t, 0)
                            up(t, 1)
                            turn_att(t + 1, 1)
                            turn_norm(t + 1, 0)
                            down(t, 1)
                            out_proj(t + 1, 1)
                            sum_group(t, 1)
                            turn_norm(t + 1, 1)
                end_phase()

        def finish():
            with ExitStack() as ph:
                wsum_s = sb(ph, "wsum_s", [P, D])
                bsum_b = sb(ph, "bsum_b", [P, D])
                wb = sb(ph, "wb", [2, 2, D])
                vecs = sb(ph, "vecs", [2, 2, 2, P])
                xin = sb(ph, "xin", [P, 2, D])
                hin = sb(ph, "hin", [P, 2, D])
                sin = sb(ph, "sin", [P, 2, TABLES, YW])
                x1 = sb(ph, "x1", [P, 2, D])
                pair = sb(ph, "pair", [P, 2, 2, YW])
                tot = sb(ph, "tot", [P, 2, YW])
                totT = sb(ph, "totT", [P, 2, P])
                ideg = sb(ph, "ideg", [P, 2, 2], i32)
                zi = sb(ph, "zi", [P, 2, D])
                zo = sb(ph, "zo", [P, 2, D])
                sg = sb(ph, "sg", [P, 2, 2 * D])
                st = sb(ph, "st", [P, 2, 6])
                mv = sb(ph, "mv", [P, 2, 2])
                veps = sb(ph, "veps", [P, 2, 1])
                rs = sb(ph, "rs", [P, 2, 1])
                xn = sb(ph, "xn", [P, 2, D])
                acc = sb(ph, "acc", [P, 2, 5, D])
                zz = sb(ph, "zz", [P, 2, D])
                sv = sb(ph, "sv", [P, 2, D])
                sg_p = [pb(ph, f"sg_p{k}") for k in range(2)]
                t_p = [pb(ph, f"t_p{k}") for k in range(2)]
                s_p = [pb(ph, f"s_p{k}") for k in range(2)]
                s = Names(pool)
                w_in_s, ones_s, pool_go, aggr_go = s.many(4)
                n_in, s_in, c_in, x1_s, st_s, mv_s, ve_s, rs_s, deg_s, tot_s = (s.many(2) for _ in range(10))
                zz_s, sv_s, tt_s, tc_s, sp_s, sgm_s, sga_s, o_c, o_s, stored, p_c = (s.many(2) for _ in range(11))

                with nc.Block() as block:
                    @block.sync
                    def _(sp):
                        sp.wait_ge(ones_s, 1)
                        sp.dma_start(wsum_s[:, :], w_sum).then_inc(w_in_s, 16)
                        sp.dma_start(bsum_b[:, :], b_sum.rearrange("(a n) -> a n", a=1).to_broadcast([P, D])).then_inc(w_in_s, 16)
                        for j, (w, b) in enumerate(((w_cent, b_cent), (w_vor, b_vor))):
                            sp.dma_start(wb[0:1, j, :], w).then_inc(w_in_s, 16)
                            sp.dma_start(wb[1:2, j, :], b.rearrange("(a n) -> a n", a=1)).then_inc(w_in_s, 16)
                        with sp.Fori(0, PAIRS) as t:
                            for k in range(2):
                                n = t * 2 + k
                                x_n, h_n = rows(x, n), rows(Hd, n)
                                sum_n = [rows(sum_d[r], n) for r in range(TABLES)]
                                vec_n = [vec[bass.ds(n, 1), :] for vec in (cent_v, vor_v)]
                                sp.wait_ge(sgm_s[k], t)
                                for j in range(2):
                                    sp.dma_start(vecs[0:1, k, j, :], vec_n[j]).then_inc(c_in[k], 16)
                                sp.wait_ge(x1_s[k], t)
                                sp.dma_start(xin[:, k, :], x_n).then_inc(n_in[k], 16)
                                sp.dma_start(hin[:, k, :], h_n).then_inc(n_in[k], 16)
                                sp.wait_ge(p_c[k], t * 2)
                                for r in range(TABLES):
                                    sp.dma_start(sin[:, k, r, :], sum_n[r]).then_inc(s_in[k], 16)

                    @block.gpsimd
                    def _(g):
                        with g.Fori(0, PAIRS) as t:
                            for k in range(2):
                                g.wait_ge(ve_s[k], t + 1)
                                g.tensor_tensor(out=rs[:, k, :], in0=veps[:, k, :], in1=neghalf[:, :], op=ALU.pow).then_inc(rs_s[k], 1)
                                g.wait_ge(deg_s[k], t + 1)
                                g.wait_ge(zz_s[k], t)
                                g.sem_inc(pool_go, 1)
                                for j, (buf, table) in enumerate(((zi, z_in), (zo, z_out))):
                                    g.indirect_dma_start(out=buf[:, k, :], out_offset=None, in_=table,
                                                         in_offset=bass.IndirectOffsetOnAxis(ap=ideg[:, k, j:j + 1], axis=0)
                                                         ).then_inc(zi_s[k], 16)
                            for k in range(2):
                                g.wait_ge(sga_s[k], t + 1)
                                g.wait_ge(o_s[k], t)
                                g.tensor_tensor(out=sv[:, k, :], in0=sg[:, k, 0:D], in1=sg[:, k, D:2 * D], op=ALU.add).then_inc(sv_s[k], 1)
                                g.wait_ge(zi_s[k], t * 32 + 32)
                                g.tensor_tensor(out=zz[:, k, :], in0=zi[:, k, :], in1=zo[:, k, :], op=ALU.add).then_inc(zz_s[k], 1)

                    @block.vector
                    def _(v):
                        v.memset(vecs[:, :, :, :], 1.0).then_inc(ones_s, 1)

                        def start(t, k):
                            n = t * 2 + k
                            v.wait_ge(n_in[k], t * 32 + 32)
                            v.tensor_tensor(out=x1[:, k, :], in0=xin[:, k, :], in1=hin[:, k, :], op=ALU.add).then_inc(x1_s[k], 1)
                            v.wait_ge(s_in[k], t * 64 + 64)
                            v.wait_ge(tt_s[k], t)
                            v.tensor_tensor(out=pair[:, k, 0, :], in0=sin[:, k, 0, :], in1=sin[:, k, 1, :], op=ALU.add).then_inc(p_c[k], 1)
                            v.tensor_tensor(out=pair[:, k, 1, :], in0=sin[:, k, 2, :], in1=sin[:, k, 3, :], op=ALU.add).then_inc(p_c[k], 1)
                            v.wait_ge(x1_s[k], t + 1)
                            v.bn_stats(out=st[:, k, :], in_=x1[:, k, :]).then_inc(st_s[k], 1)
                            v.wait_ge(p_c[k], t * 2 + 2)
                            v.tensor_tensor(out=tot[:, k, :], in0=pair[:, k, 0, :], in1=pair[:, k, 1, :], op=ALU.add).then_inc(tot_s[k], 1)
                            v.wait_ge(st_s[k], t + 1)
                            v.sem_inc(aggr_go, 1)
                            v.bn_aggr(out=mv[:, k, :], in_=st[:, k, :]).then_inc(mv_s[k], 1)
                            v.wait_ge(zi_s[k], t * 32)
                            v.tensor_scalar(out=ideg[:, k, 0:1], in0=region[:, bass.ds(n * XW + D + 2 * H, 1)],
                                            scalar1=float(MAX_DEG), scalar2=None, op0=ALU.min)
                            v.wait_ge(mv_s[k], t + 1)
                            v.tensor_scalar(out=veps[:, k, :], in0=mv[:, k, 1:2], scalar1=EPS, scalar2=None,
                                            op0=ALU.add).then_inc(ve_s[k], 1)
                            v.wait_ge(tot_s[k], t + 1)
                            v.tensor_scalar(out=ideg[:, k, 1:2], in0=tot[:, k, ED:ED + 1], scalar1=float(MAX_DEG),
                                            scalar2=None, op0=ALU.min).then_inc(deg_s[k], 1)

                        def total(t, k):
                            c = t * 5
                            v.wait_ge(rs_s[k], t + 1)
                            v.wait_ge(stored[k], t * 16)
                            v.tensor_scalar(out=xn[:, k, :], in0=x1[:, k, :], scalar1=mv[:, k, 0:1], scalar2=rs[:, k, :],
                                            op0=ALU.subtract, op1=ALU.mult).then_inc(o_c[k], 1)
                            v.wait_ge(sp_s[k], t + 1)
                            v.scalar_tensor_tensor(out=acc[:, k, 0, :], in0=bsum_b[:, :], scalar=tot[:, k, ED:ED + 1],
                                                   in1=s_p[k][:, 0:D], op0=ALU.mult, op1=ALU.add).then_inc(o_c[k], 1)
                            v.wait_ge(o_c[k], c + 1)
                            v.scalar_tensor_tensor(out=acc[:, k, 1, :], in0=xn[:, k, :], scalar=0.0, in1=x1[:, k, :],
                                                   op0=ALU.max, op1=ALU.add).then_inc(o_c[k], 1)
                            v.wait_ge(sv_s[k], t + 1)
                            v.wait_ge(o_c[k], c + 2)
                            v.tensor_tensor(out=acc[:, k, 2, :], in0=acc[:, k, 0, :], in1=sv[:, k, :], op=ALU.add).then_inc(o_c[k], 1)
                            v.wait_ge(zz_s[k], t + 1)
                            v.wait_ge(o_c[k], c + 3)
                            v.tensor_tensor(out=acc[:, k, 3, :], in0=acc[:, k, 1, :], in1=zz[:, k, :], op=ALU.add).then_inc(o_c[k], 1)
                            v.wait_ge(o_c[k], c + 5)
                            v.tensor_tensor(out=acc[:, k, 4, :], in0=acc[:, k, 2, :], in1=acc[:, k, 3, :], op=ALU.add).then_inc(o_s[k], 1)

                        v.wait_ge(w_in_s, 16 * 6)
                        with v.Fori(0, PAIRS) as t:
                            for k in range(2):
                                start(t, k)
                            for k in range(2):
                                total(t, k)

                    @block.scalar
                    def _(a):
                        with a.Fori(0, PAIRS) as t:
                            for k in range(2):
                                a.wait_ge(tt_s[k], t + 1)
                                a.wait_ge(sp_s[k], t)
                                a.activation(totT[:, k, :], t_p[k][:, 0:P], ACT.Copy).then_inc(tc_s[k], 1)
                                a.wait_ge(sgm_s[k], t + 1)
                                a.wait_ge(sv_s[k], t)
                                a.activation(sg[:, k, :], sg_p[k][:, :], ACT.Sigmoid).then_inc(sga_s[k], 1)
                            for k in range(2):
                                a.wait_ge(o_s[k], t + 1)
                                a.dma_start(rows(out, t * 2 + k), acc[:, k, 4, :]).then_inc(stored[k], 16)
                        for k in range(2):
                            a.wait_ge(stored[k], 16 * PAIRS)

                    @block.tensor
                    def _(pe):
                        pe.wait_ge(w_in_s, 16 * 6)
                        with pe.Fori(0, PAIRS) as t:
                            for k in range(2):
                                pe.wait_ge(c_in[k], t * 32 + 32)
                                pe.wait_ge(sga_s[k], t)
                                for j in range(2):
                                    ins = pe.matmul(sg_p[k][:, j * D:(j + 1) * D], vecs[:, k, j, :], wb[:, j, :], start=True, stop=True)
                                ins.then_inc(sgm_s[k], 1)
                                pe.wait_ge(tot_s[k], t + 1)
                                pe.wait_ge(tc_s[k], t)
                                pe.transpose(t_p[k][:, 0:P], tot[:, k, 0:P], ident[:, :]).then_inc(tt_s[k], 1)
                            for k in range(2):
                                pe.wait_ge(tc_s[k], t + 1)
                                pe.wait_ge(o_s[k], t)
                                pe.matmul(s_p[k][:, 0:D], totT[:, k, :], wsum_s[:, :], start=True, stop=True).then_inc(sp_s[k], 1)
                end_phase()

        project(-1)
        for l in range(L):
            project(l)
            with ExitStack() as edges:
                S = sb(edges, "S", [P, 2 * H, NI])
                edge_scores(S, 2 * l * 16 * TURNS)
                edge_weights(S)
                edge_sums(S, (2 * l + 1) * 16 * TURNS)
            update(l)
        finish()


def kernel(**inputs):
    import numpy as np
    import concourse.bacc as bacc
    from concourse.bass_utils import run_bass_kernel_spmd as run

    def padded(a, shape, fill=0):
        out = np.full(shape, fill, a.dtype)
        out[tuple(slice(0, n) for n in a.shape)] = a
        return out

    a = {name: np.asarray(v) for name, v in inputs.items()}
    groups = GROUPS + 2
    src, dst = a["src"], a["dst"]
    by_group = padded(src, (groups * EG * P,), N).reshape(groups, P, EG)
    arrays = {
        "x": padded(a["x"], (NPA, D)),
        "src_items": padded(src, ((ET + 1) * P,), N).reshape(ET + 1, P),
        "dst_items": padded(dst, ((ET + 1) * P,), SENTINEL).reshape(ET + 1, P),
        "src_rows": np.ascontiguousarray(by_group.transpose(0, 2, 1)).reshape(groups, EG * P),
        "src_cols": by_group.reshape(groups * P, EG),
        "edge_attr": padded(a["edge_attr_128"], (groups * EG * P, ED)).reshape(groups * P, EG * ED),
        "vor_v": padded(a["node_vec1"], (NPA, 1)).reshape(NTA, P),
        "cent_v": padded(a["node_vec1_n2"], (NPA, 1)).reshape(NTA, P),
    }
    for name in ("w_in", "b_in", "ln1_g", "ln1_b", "ln2_g", "ln2_b", "wq", "bq", "wk", "bk", "wv", "bv",
                 "wo", "bo", "w1", "b1", "w2", "b2"):
        arrays[name] = np.ascontiguousarray(a[f"L0_gnn_{name}"])
    for name in ("z_in", "z_out", "W_cent", "b_cent", "W_vor", "b_vor", "W_sum", "b_sum"):
        arrays[name] = np.ascontiguousarray(a[f"L1_gnn_{name}"])

    nc = bacc.Bacc("TRN2", target_bir_lowering=False, num_devices=1)
    args = [nc.dram_tensor(f"in_{n}", v.shape, mybir.dt.from_np(v.dtype), kind="ExternalInput").ap()
            for n, v in arrays.items()]
    args.append(nc.dram_tensor("out_0", (NP, D), f32, kind="ExternalOutput").ap())
    gnn_kernel(nc, *args)
    r = run(nc, [{f"in_{n}": v for n, v in arrays.items()}], core_ids=[0])
    return r.results[0]["out_0"][0:N]
```

```python
import concourse.bass as bass
from concourse import mybir
from contextlib import ExitStack

f32 = mybir.dt.float32
bf16 = mybir.dt.bfloat16
i32 = mybir.dt.int32
ALU = mybir.AluOpType
ACT = mybir.ActivationFunctionType
AX = mybir.AxisListType

P = 128
N = 6250
E = 100000
D = 256
H = 8
DH = D // H
FF = 1024
L = 2
ED = 128
EPS = 1e-5
SCALE = float(DH) ** -0.5
MAX_DEG = 511

ET = -(-E // P)
LAST = E - 1 - (ET - 1) * P
NT = 50
NTA = NT + 4
NP = NT * P
NPA = NTA * P
PAIRS = NT // 2
PT = ET // 2
GB = 8
UB = 2 * GB
NB = 56
NG = NB * GB
NI = NB * UB
IC = NI // P
RW = P + 1
CW = 3 * P
BIG = 2.0 ** 126
QW = D + H
XW = D + 2 * H + 1
EG = 8
GROUPS = L * NT
YW = ED + 4
TABLES = 4
DUMMY = NP - P
SENTINEL = 1 << 20
assert NG >= PT + -(-N // P) - 1 and ET % 2 == 0 and NB % 2 == 0 and UB * H == P and NI % P == 0
assert GROUPS * EG * P >= E and DUMMY >= N


class Names:

    def __init__(self, pool):
        self.pool = list(pool)

    def one(self):
        return self.pool.pop(0)

    def many(self, n):
        return [self.pool.pop(0) for _ in range(n)]


def gnn_kernel(nc, x, src_tiles, dst_tiles, src_rows, src_cols, edge_attr, vor_v, cent_v,
               w_in, b_in, ln1_g, ln1_b, ln2_g, ln2_b, wq, bq, wk, bk, wv, bv, wo, bo,
               w1, b1, w2, b2, z_in, z_out, w_cent, b_cent, w_vor, b_vor, w_sum, b_sum, out):
    Hd = nc.dram_tensor("h_scratch", [NPA, D], f32).ap()
    KVd = nc.dram_tensor("kv_scratch", [NPA, 2 * D], f32).ap()
    drel_d = nc.dram_tensor("drel_scratch", [NI * P], f32).ap()
    key_t = nc.dram_tensor("key_scratch", [NI * P + 2], f32)
    key_d = key_t.ap()
    nt_d = nc.dram_tensor("nt_scratch", [NI], i32).ap()
    src_d = nc.dram_tensor("src_scratch", [P, NI], i32).ap()
    ndrel_d = nc.dram_tensor("ndrel_scratch", [P, NI], f32).ap()
    reset_d = nc.dram_tensor("reset_scratch", [NB * P, RW], bf16).ap()
    chain_d = nc.dram_tensor("chain_scratch", [NB, CW], f32).ap()
    sum_d = [nc.dram_tensor(f"sum_scratch{r}", [NP, YW], f32).ap() for r in range(TABLES)]

    ctx = ExitStack()
    pool = [ctx.enter_context(nc.semaphore(f"sem{n}")) for n in range(96)]
    rows_in = ctx.enter_context(nc.semaphore("rows_in"))
    ring_in = [ctx.enter_context(nc.semaphore(f"ring_in{n}")) for n in range(2 * UB)]
    sc_s = [[ctx.enter_context(nc.semaphore(f"scatter{k}_{r}")) for r in range(TABLES)] for k in range(2)]
    zi_s = [ctx.enter_context(nc.semaphore(f"z_in{k}")) for k in range(2)]

    phase = [0]

    def sb(where, name, shape, dt=f32):
        return where.enter_context(nc.sbuf_tensor(f"{name}_{phase[0]}", shape, dt))

    def pb(where, name):
        return where.enter_context(nc.psum_tensor(f"{name}_{phase[0]}", [P, 512], f32))

    def end_phase():
        nc.gpsimd.sem_clear(range(pool[0].num, pool[-1].num + 1))
        nc.all_engine_barrier()
        phase[0] += 1

    with ctx:
        ident = sb(ctx, "ident", [P, P])
        iota_f = sb(ctx, "iota_f", [P, P])
        iota_p = sb(ctx, "iota_p", [P, 1])
        neghalf = sb(ctx, "neghalf", [P, 1])
        ones = sb(ctx, "ones", [P, P])
        nt_row = sb(ctx, "nt_row", [1, NG], i32)
        sums = sb(ctx, "sums", [P, NT * XW])

        with ExitStack() as ph:
            last_i = sb(ph, "last_i", [1, PT], i32)
            last_h = sb(ph, "last_h", [1, PT], i32)
            last_f = sb(ph, "last_f", [1, PT])
            tile_no = sb(ph, "tile_no", [1, PT])
            bound = sb(ph, "bound", [1, PT])
            bound_b = sb(ph, "bound_b", [P, PT])
            junk = sb(ph, "junk", [P, PT])
            unit_no = sb(ph, "unit_no", [P, IC])
            unit_i = sb(ph, "unit_i", [P, IC], i32)
            group_i = sb(ph, "group_i", [P, IC], i32)
            group = sb(ph, "group", [P, IC])
            which = sb(ph, "which", [P, IC])
            pt = sb(ph, "pt", [P, IC])
            et = sb(ph, "et", [P, IC])
            nt = sb(ph, "nt", [P, IC])
            base = sb(ph, "base", [P, IC])
            et_i = sb(ph, "et_i", [P, IC], i32)
            nt_i = sb(ph, "nt_i", [P, IC], i32)
            drow = sb(ph, "drow", [P, IC, P], i32)
            srow = sb(ph, "srow", [P, IC, P], i32)
            srow_f = sb(ph, "srow_f", [P, IC, P])
            drel = sb(ph, "drel", [P, IC, P])
            ge0 = sb(ph, "ge0", [P, IC, P])
            valid = sb(ph, "valid", [P, IC, P])
            key = sb(ph, "key", [P, IC, P])
            src_t = sb(ph, "src_t", [P, NI], i32)
            ndrel_t = sb(ph, "ndrel_t", [P, NI])
            guard = sb(ph, "guard", [1, 1])
            zero = sb(ph, "zero", [P, (NTA - NT) * D])
            b0, tr0, tr1 = pb(ph, "b0"), pb(ph, "tr0"), pb(ph, "tr1")
            s = Names(pool)
            last_in, consts, sel_base, bound_done, bc_done, tables = s.many(6)
            drel_done, key_done, srcf_done, tr_done, tr_out, stored, nt_stored, nt_in, dve_c, zeroed, z_out_s, grp = s.many(12)
            with nc.Block() as block:
                @block.sync
                def _(sp):
                    sp.dma_start(last_i[0:1, 0:PT - 1],
                                 dst_tiles[1:ET - 1:2, P - 1:P].rearrange("t o -> o t"),
                                 allow_slow_non_contiguous=True).then_inc(last_in, 16)
                    sp.dma_start(last_i[0:1, PT - 1:PT],
                                 dst_tiles[ET - 1:ET, LAST:LAST + 1]).then_inc(last_in, 16)
                    sp.wait_ge(zeroed, 1)
                    for d in (Hd, KVd[:, 0:D], KVd[:, D:2 * D]):
                        sp.dma_start(d[NP:NPA, :].rearrange("(p a) d -> p a d", p=P),
                                     zero[:, :].rearrange("p (a d) -> p a d", d=D)).then_inc(z_out_s, 16)
                    sp.wait_ge(tables, 2)
                    sp.dma_start(nt_d.rearrange("(c p) -> p c", p=P), nt_i[:, :],
                                 allow_slow_non_contiguous=True).then_inc(nt_stored, 16)
                    sp.wait_ge(nt_stored, 16)
                    sp.dma_start(nt_row[0:1, :].unsqueeze(2), nt_d.rearrange("(a n j) -> a n j", a=1, j=2)[:, :, 0:1],
                                 allow_slow_non_contiguous=True).then_inc(nt_in, 16)
                    sp.wait_ge(drel_done, 1)
                    sp.dma_start(drel_d.rearrange("(c p e) -> p c e", p=P, e=P), drel[:, :, :]).then_inc(stored, 16)
                    sp.wait_ge(key_done, 1)
                    sp.dma_start(key_d[1:1 + NI * P].rearrange("(c p e) -> p c e", p=P, e=P),
                                 key[:, :, :]).then_inc(stored, 16)
                    for at in (0, NI * P + 1):
                        sp.dma_start(key_d[at:at + 1].rearrange("(a n) -> a n", a=1), guard[:, :]).then_inc(stored, 16)
                    sp.wait_ge(tr_out, IC)
                    sp.dma_start(src_d, src_t[:, :]).then_inc(stored, 16)
                    sp.dma_start(ndrel_d, ndrel_t[:, :]).then_inc(stored, 16)
                    sp.wait_ge(nt_in, 16)
                    sp.wait_ge(stored, 16 * 6)
                    sp.wait_ge(z_out_s, 48)

                @block.gpsimd
                def _(g):
                    g.memset(ident[:, :], 0.0).then_inc(sel_base, 1)
                    g.memset(ones[:, :], 1.0)
                    g.memset(neghalf[:, :], -0.5)
                    g.memset(guard[:, :], -1.0)
                    g.iota(iota_f[:, :], [[1, P]], base=0, channel_multiplier=0,
                           allow_small_or_imprecise_dtypes=True)
                    g.iota(iota_p[:, :], [[0, 1]], base=0, channel_multiplier=1,
                           allow_small_or_imprecise_dtypes=True)
                    g.iota(tile_no[:, :], [[1, PT]], base=0, channel_multiplier=0,
                           allow_small_or_imprecise_dtypes=True)
                    g.iota(unit_no[:, :], [[P, IC]], base=0, channel_multiplier=1,
                           allow_small_or_imprecise_dtypes=True)
                    g.iota(unit_i[:, :], [[P, IC]], base=0, channel_multiplier=1)
                    g.wait_ge(sel_base, 1)
                    g.affine_select(out=ident[:, :], in_=ident[:, :], compare_op=ALU.not_equal, fill=1.0,
                                    base=0, pattern=[[-1, P]], channel_multiplier=1).then_inc(consts, 1)
                    g.wait_ge(tables, 1)
                    for c in range(IC):
                        off = bass.IndirectOffsetOnAxis(ap=et_i[:, c:c + 1], axis=0)
                        g.indirect_dma_start(out=drow[:, c, :], out_offset=None, in_=dst_tiles,
                                             in_offset=off).then_inc(rows_in, 16)
                        g.indirect_dma_start(out=srow[:, c, :], out_offset=None, in_=src_tiles,
                                             in_offset=off).then_inc(rows_in, 16)
                    g.wait_ge(rows_in, 32 * IC)

                @block.vector
                def _(v):
                    v.memset(zero[:, :], 0.0).then_inc(zeroed, 1)
                    v.wait_ge(last_in, 32)
                    v.tensor_scalar(out=last_h[:, :], in0=last_i[:, :], scalar1=7, scalar2=None,
                                    op0=ALU.arith_shift_right).then_inc(dve_c, 1)
                    v.wait_ge(dve_c, 1)
                    v.tensor_copy(last_f[:, :], last_h[:, :]).then_inc(dve_c, 1)
                    v.wait_ge(dve_c, 2)
                    v.wait_ge(consts, 1)
                    v.tensor_tensor(out=bound[:, :], in0=last_f[:, :], in1=tile_no[:, :],
                                    op=ALU.add).then_inc(bound_done, 1)
                    v.tensor_scalar(out=group_i[:, :], in0=unit_i[:, :], scalar1=1, scalar2=None,
                                    op0=ALU.arith_shift_right).then_inc(grp, 1)
                    v.wait_ge(grp, 1)
                    v.tensor_copy(group[:, :], group_i[:, :]).then_inc(grp, 1)
                    v.wait_ge(grp, 2)
                    v.scalar_tensor_tensor(out=which[:, :], in0=group[:, :], scalar=-2.0, in1=unit_no[:, :],
                                           op0=ALU.mult, op1=ALU.add).then_inc(grp, 1)
                    v.wait_ge(bc_done, 1)
                    v.tensor_copy(bound_b[:, :], b0[:, 0:PT]).then_inc(dve_c, 1)
                    v.wait_ge(dve_c, 3)
                    for c in range(IC):
                        if c >= 1:
                            v.wait_ge(dve_c, 3 + c)
                        v.tensor_scalar(out=junk[:, :], in0=bound_b[:, :], scalar1=group[:, c:c + 1],
                                        scalar2=None, op0=ALU.is_lt, op1=ALU.add,
                                        accum_out=pt[:, c:c + 1]).then_inc(dve_c, 1)
                    v.wait_ge(dve_c, 3 + IC)
                    v.wait_ge(grp, 3)
                    v.scalar_tensor_tensor(out=et[:, :], in0=pt[:, :], scalar=2.0, in1=which[:, :],
                                           op0=ALU.mult, op1=ALU.add).then_inc(grp, 1)
                    v.wait_ge(grp, 4)
                    v.tensor_copy(et_i[:, :], et[:, :]).then_inc(tables, 1)
                    v.tensor_tensor(out=nt[:, :], in0=group[:, :], in1=pt[:, :],
                                    op=ALU.subtract).then_inc(dve_c, 1)
                    v.wait_ge(dve_c, 4 + IC)
                    v.tensor_scalar(out=base[:, :], in0=nt[:, :], scalar1=float(P), scalar2=None,
                                    op0=ALU.mult).then_inc(dve_c, 1)
                    v.tensor_scalar(out=nt_i[:, :], in0=nt[:, :], scalar1=float(NT - 1), scalar2=None,
                                    op0=ALU.min).then_inc(tables, 1)
                    v.wait_ge(dve_c, 5 + IC)
                    v.wait_ge(rows_in, 32 * IC)
                    for c in range(IC):
                        ins = v.tensor_scalar(out=drel[:, c, :], in0=drow[:, c, :], scalar1=base[:, c:c + 1],
                                              scalar2=None, op0=ALU.subtract)
                    ins.then_inc(drel_done, 1)
                    v.tensor_copy(srow_f[:, :, :], srow[:, :, :]).then_inc(srcf_done, 1)
                    v.wait_ge(drel_done, 1)
                    v.tensor_scalar(out=ge0[:, :, :], in0=drel[:, :, :], scalar1=0.0, scalar2=None,
                                    op0=ALU.is_ge).then_inc(dve_c, 1)
                    v.wait_ge(dve_c, 6 + IC)
                    v.scalar_tensor_tensor(out=valid[:, :, :], in0=drel[:, :, :], scalar=float(P),
                                           in1=ge0[:, :, :], op0=ALU.is_lt, op1=ALU.mult).then_inc(dve_c, 1)
                    v.wait_ge(dve_c, 7 + IC)
                    v.scalar_tensor_tensor(out=key[:, :, :], in0=drow[:, :, :], scalar=1.0,
                                           in1=valid[:, :, :], op0=ALU.add, op1=ALU.mult).then_inc(key_done, 1)
                    for c in range(IC):
                        v.wait_ge(tr_done, c + 1)
                        cols = slice(c * P, (c + 1) * P)
                        v.tensor_scalar(out=ndrel_t[:, cols], in0=(tr0, tr1)[c % 2][:, 0:P], scalar1=-1.0,
                                        scalar2=None, op0=ALU.mult)
                        v.tensor_copy(src_t[:, cols], (tr0, tr1)[c % 2][:, P:2 * P]).then_inc(tr_out, 1)

                @block.tensor
                def _(pe):
                    pe.wait_ge(consts, 1)
                    pe.wait_ge(bound_done, 1)
                    pe.matmul(b0[:, 0:PT], ones[0:1, :], bound[0:1, :], start=True, stop=True).then_inc(bc_done, 1)
                    pe.wait_ge(drel_done, 1)
                    pe.wait_ge(srcf_done, 1)
                    for c in range(IC):
                        if c >= 2:
                            pe.wait_ge(tr_out, c - 1)
                        bank = (tr0, tr1)[c % 2]
                        pe.transpose(bank[:, 0:P], drel[:, c, :], ident[:, :])
                        pe.transpose(bank[:, P:2 * P], srow_f[:, c, :], ident[:, :]).then_inc(tr_done, 1)
            end_phase()

        with ExitStack() as ph:
            win = sb(ph, "win", [P, NB, P + 2])
            ne = sb(ph, "ne", [P, NB, RW])
            resets = sb(ph, "resets", [P, NB, RW], bf16)
            has = sb(ph, "has", [P, 2, NB])
            first_key = sb(ph, "first_key", [NB, 2])
            first_drel = sb(ph, "first_drel", [NB, 1])
            goes_on = sb(ph, "goes_on", [NB, 1])
            chain = sb(ph, "chain", [NB, CW])
            zeros = sb(ph, "zeros", [P, 10 * YW])
            cp = pb(ph, "cp")
            s = Names(pool)
            keys_in, first_in, ne_s, res_s, red, trn, row_s, ch_s, zr, z_done = s.many(10)
            with nc.Block() as block:
                @block.sync
                def _(sp):
                    for h in range(H):
                        sp.dma_start(win[h * UB:(h + 1) * UB, :, :],
                                     bass.AP(key_t, 0, [[P, UB], [UB * P, NB], [1, P + 2]])).then_inc(keys_in, 16)
                    sp.dma_start(first_key[:, :], bass.AP(key_t, 0, [[UB * P, NB], [1, 2]])).then_inc(first_in, 16)
                    sp.dma_start(first_drel[:, :], drel_d.rearrange("(b j) -> b j", b=NB)[:, 0:1],
                                 allow_slow_non_contiguous=True).then_inc(first_in, 16)
                    sp.wait_ge(zr, 1)
                    for r in range(TABLES):
                        for q in range(5):
                            sp.dma_start(sum_d[r][q * 10 * P:(q + 1) * 10 * P, :].rearrange("(p a) w -> p (a w)", p=P),
                                         zeros[:, :]).then_inc(z_done, 16)
                    sp.wait_ge(res_s, 1)
                    sp.dma_start(reset_d.rearrange("(b p) e -> p b e", p=P), resets[:, :, :]).then_inc(z_done, 16)
                    sp.wait_ge(ch_s, 2)
                    sp.dma_start(chain_d, chain[:, :]).then_inc(z_done, 16)
                    sp.wait_ge(z_done, 16 * (5 * TABLES + 2))

                @block.vector
                def _(v):
                    v.memset(zeros[:, :], 0.0).then_inc(zr, 1)
                    v.wait_ge(keys_in, 16 * H)
                    v.tensor_tensor(out=ne[:, :, :], in0=win[:, :, 1:P + 2], in1=win[:, :, 0:RW],
                                    op=ALU.not_equal).then_inc(ne_s, 1)
                    v.wait_ge(ne_s, 1)
                    v.tensor_scalar(out=resets[:, :, :], in0=ne[:, :, :], scalar1=-BIG, scalar2=None,
                                    op0=ALU.mult).then_inc(res_s, 1)
                    v.tensor_reduce(out=has[:, 0, :], in_=ne[:, :, 0:P], axis=AX.X, op=ALU.max)
                    v.tensor_reduce(out=has[:, 1, :], in_=ne[:, :, 1:RW], axis=AX.X, op=ALU.max).then_inc(red, 1)
                    v.wait_ge(first_in, 32)
                    v.tensor_tensor(out=goes_on[:, :], in0=first_key[:, 0:1], in1=first_key[:, 1:2],
                                    op=ALU.is_equal).then_inc(row_s, 1)
                    v.wait_ge(row_s, 1)
                    v.tensor_scalar(out=chain[:, 2 * P:CW], in0=iota_f[0:NB, :], scalar1=first_drel[:, 0:1],
                                    scalar2=goes_on[:, 0:1], op0=ALU.is_equal, op1=ALU.mult)
                    v.wait_ge(trn, 1)
                    v.tensor_scalar(out=chain[:, 0:2 * P], in0=cp[0:NB, 0:2 * P], scalar1=-BIG, scalar2=None,
                                    op0=ALU.mult).then_inc(ch_s, 1)
                    v.wait_ge(ch_s, 1)
                    v.memset(chain[:, 0:P:UB], -BIG)
                    v.memset(chain[:, P + UB - 1:2 * P:UB], -BIG).then_inc(ch_s, 1)

                @block.tensor
                def _(pe):
                    pe.wait_ge(red, 1)
                    pe.transpose(cp[0:NB, 0:P], has[:, 0, :], ident[:, :])
                    pe.transpose(cp[0:NB, P:2 * P], has[:, 1, :], ident[:, :]).then_inc(trn, 1)
            end_phase()
        def rows(d, n):
            return d[bass.ds(n * P, P), :]

        def project(l, queries=None):
            first = l < 0
            W = D if first else 3 * D
            src = x if first else Hd
            with ExitStack() as ph:
                w = sb(ph, "w", [P, 2, W])
                bias = sb(ph, "bias", [P, W])
                gcol = sb(ph, "gcol", [P, 2])
                bcol = sb(ph, "bcol", [P, 2])
                bmat = sb(ph, "bmat", [P, 2, P])
                hin = sb(ph, "hin", [P, 2, D])
                st = sb(ph, "st", [P, 2, 6])
                mv = sb(ph, "mv", [P, 2, 2])
                veps = sb(ph, "veps", [P, 2, 1])
                rs = sb(ph, "rs", [P, 2, 1])
                xn = sb(ph, "xn", [P, 2, D])
                xT = sb(ph, "xT", [P, 2, D])
                res = sb(ph, "res", [P, 2, W])
                qk = sb(ph, "qk", [P, 2, D])
                tp = [pb(ph, f"tp{k}") for k in range(2)]
                mma = [pb(ph, f"mma{k}") for k in range(2)]
                mmb = [pb(ph, f"mmb{k}") for k in range(2)]
                s = Names(pool)
                w_in_s, bm, wf, bias_mm, bias_ok, aggr_go = s.many(6)
                h_in, st_s, mv_s, ve_s, rs_s, xn_s, tr_s, xt_s, mm_s, ev_s, pr_s, rd_s, kv_out = (s.many(2) for _ in range(13))

                with nc.Block() as block:
                    @block.sync
                    def _(sp):
                        if first:
                            sp.dma_start(w[:, :, :], w_in.rearrange("(c p) n -> p c n", p=P)).then_inc(w_in_s, 16)
                            sp.dma_start(bias[:, :], b_in.rearrange("(a n) -> a n", a=1).to_broadcast([P, D])).then_inc(w_in_s, 16)
                        else:
                            for j, (m, b) in enumerate(((wq, bq), (wk, bk), (wv, bv))):
                                cols = slice(j * D, (j + 1) * D)
                                sp.dma_start(w[:, :, cols], m[l].rearrange("(c p) n -> p c n", p=P)).then_inc(w_in_s, 16)
                                sp.dma_start(bias[:, cols], b[l:l + 1, :].to_broadcast([P, D])).then_inc(w_in_s, 16)
                            sp.dma_start(gcol[:, :], ln1_g[l].rearrange("(c p) -> p c", p=P),
                                         allow_slow_non_contiguous=True).then_inc(w_in_s, 16)
                            sp.dma_start(bcol[:, :], ln1_b[l].rearrange("(c p) -> p c", p=P),
                                         allow_slow_non_contiguous=True).then_inc(w_in_s, 16)
                        with sp.Fori(0, PAIRS) as t:
                            for k in range(2):
                                sp.wait_ge(ev_s[k], t + 1)
                                if first:
                                    sp.dma_start(rows(Hd, t * 2 + k), res[:, k, :]).then_inc(kv_out[k], 16)
                                else:
                                    sp.dma_start(rows(KVd, t * 2 + k), res[:, k, D:W]).then_inc(kv_out[k], 16)
                        for k in range(2):
                            sp.wait_ge(kv_out[k], 16 * PAIRS)

                    def load(a, t, k):
                        a.wait_ge(xn_s[k], t)
                        a.dma_start(hin[:, k, :], rows(src, t * 2 + k)).then_inc(h_in[k], 16)

                    @block.scalar
                    def _(a):
                        def turned(t, k):
                            a.wait_ge(tr_s[k], t + 1)
                            a.wait_ge(mm_s[k], t)
                            a.activation(xT[:, k, :], tp[k][:, 0:D], ACT.Relu if first else ACT.Copy).then_inc(xt_s[k], 1)

                        for k in range(2):
                            load(a, 0, k)
                        for k in range(2):
                            load(a, 1, k)
                            turned(0, k)
                        with a.Fori(0, PAIRS) as t:
                            for k in range(2):
                                load(a, t + 2, k)
                                turned(t + 1, k)

                        for k in range(2):
                            a.wait_ge(h_in[k], 16 * (PAIRS + 2))

                    @block.gpsimd
                    def _(g):
                        if not first:
                            g.memset(sums[:, :], 0.0)
                        with g.Fori(0, PAIRS + 1) as t:
                            for k in range(2):
                                g.wait_ge(ve_s[k], t + 1)
                                g.tensor_tensor(out=rs[:, k, :], in0=veps[:, k, :], in1=neghalf[:, :],
                                                op=ALU.pow).then_inc(rs_s[k], 1)
                        g.wait_ge(ve_s[0], PAIRS + 2)
                        g.tensor_tensor(out=rs[:, 0, :], in0=veps[:, 0, :], in1=neghalf[:, :], op=ALU.pow).then_inc(rs_s[0], 1)

                    @block.vector
                    def _(v):
                        if not first:
                            v.wait_ge(w_in_s, 16 * 8)
                            for c in range(2):
                                ins = v.tensor_scalar(out=bmat[:, c, :], in0=ones[:, :], scalar1=bcol[:, c:c + 1],
                                                      scalar2=None, op0=ALU.mult)
                            ins.then_inc(bm, 1)
                            v.wait_ge(bias_mm, 1)
                            v.tensor_tensor(out=bias[:, 0:2 * D], in0=bias[:, 0:2 * D], in1=mma[0][:, 0:2 * D], op=ALU.add)
                            v.tensor_tensor(out=bias[:, 2 * D:W], in0=bias[:, 2 * D:W], in1=mmb[0][:, 0:D],
                                            op=ALU.add).then_inc(wf, 1)
                            for c in range(2):
                                v.tensor_scalar(out=w[:, c, 0:D], in0=w[:, c, 0:D], scalar1=gcol[:, c:c + 1],
                                                scalar2=SCALE, op0=ALU.mult, op1=ALU.mult)
                                ins = v.tensor_scalar(out=w[:, c, D:W], in0=w[:, c, D:W], scalar1=gcol[:, c:c + 1],
                                                      scalar2=None, op0=ALU.mult)
                            ins.then_inc(wf, 1)
                            v.wait_ge(wf, 1)
                            v.tensor_scalar(out=bias[:, 0:D], in0=bias[:, 0:D], scalar1=SCALE, scalar2=None,
                                            op0=ALU.mult).then_inc(bias_ok, 1)
                        else:
                            v.wait_ge(w_in_s, 32)

                        def stats(t, k):
                            v.wait_ge(h_in[k], t * 16 + 16)
                            v.wait_ge(xn_s[k], t)
                            v.bn_stats(out=st[:, k, :], in_=hin[:, k, :]).then_inc(st_s[k], 1)
                            v.wait_ge(st_s[k], t + 1)
                            v.sem_inc(aggr_go, 1)
                            v.bn_aggr(out=mv[:, k, :], in_=st[:, k, :]).then_inc(mv_s[k], 1)
                            v.wait_ge(mv_s[k], t + 1)
                            v.tensor_scalar(out=veps[:, k, :], in0=mv[:, k, 1:2], scalar1=EPS, scalar2=None,
                                            op0=ALU.add).then_inc(ve_s[k], 1)

                        def norm(t, k):
                            v.wait_ge(rs_s[k], t + 1)
                            v.wait_ge(tr_s[k], t)
                            v.tensor_scalar(out=xn[:, k, :], in0=hin[:, k, :], scalar1=mv[:, k, 0:1],
                                            scalar2=rs[:, k, :], op0=ALU.subtract, op1=ALU.mult).then_inc(xn_s[k], 1)

                        def results(t, k):
                            v.wait_ge(mm_s[k], t + 1)
                            v.wait_ge(kv_out[k], t * 16)
                            if first:
                                v.tensor_tensor(out=res[:, k, :], in0=mma[k][:, 0:D], in1=bias[:, :],
                                                op=ALU.add).then_inc(ev_s[k], 1)
                                return
                            v.tensor_tensor(out=res[:, k, 0:2 * D], in0=mma[k][:, 0:2 * D], in1=bias[:, 0:2 * D], op=ALU.add)
                            v.tensor_tensor(out=res[:, k, 2 * D:W], in0=mmb[k][:, 0:D], in1=bias[:, 2 * D:W],
                                            op=ALU.add).then_inc(ev_s[k], 1)
                            v.wait_ge(ev_s[k], t + 1)
                            v.wait_ge(rd_s[k], t)
                            at = (t * 2 + k) * QW
                            v.tensor_tensor(out=qk[:, k, :], in0=res[:, k, 0:D], in1=res[:, k, D:2 * D],
                                            op=ALU.mult).then_inc(pr_s[k], 1)
                            v.tensor_copy(queries[:, bass.ds(at, D)], res[:, k, 0:D])
                            v.wait_ge(pr_s[k], t + 1)
                            v.tensor_reduce(out=queries[:, bass.ds(at + D, H)],
                                            in_=qk[:, k, :].rearrange("p (h d) -> p h d", d=DH),
                                            axis=AX.X, op=ALU.add).then_inc(rd_s[k], 1)

                        for k in range(2):
                            stats(0, k)
                        for k in range(2):
                            norm(0, k)
                        stats(1, 0)
                        with v.Fori(0, PAIRS) as t:
                            norm(t + 1, 0)
                            stats(t + 1, 1)
                            results(t, 0)
                            norm(t + 1, 1)
                            stats(t + 2, 0)
                            results(t, 1)
                        v.wait_ge(rs_s[0], PAIRS + 2)

                    @block.tensor
                    def _(pe):
                        if not first:
                            pe.wait_ge(bm, 1)
                            for c in range(2):
                                pe.matmul(mma[0][:, 0:2 * D], bmat[:, c, :], w[:, c, 0:2 * D], start=(c == 0), stop=(c == 1))
                            for c in range(2):
                                ins = pe.matmul(mmb[0][:, 0:D], bmat[:, c, :], w[:, c, 2 * D:W], start=(c == 0), stop=(c == 1))
                            ins.then_inc(bias_mm, 1)
                            pe.wait_ge(wf, 2)
                        else:
                            pe.wait_ge(w_in_s, 32)

                        def turn(t, k):
                            pe.wait_ge(xn_s[k], t + 1)
                            pe.wait_ge(xt_s[k], t)
                            for c in range(2):
                                ins = pe.transpose(tp[k][:, c * P:(c + 1) * P], xn[:, k, c * P:(c + 1) * P], ident[:, :])
                            ins.then_inc(tr_s[k], 1)

                        def products(t, k):
                            pe.wait_ge(xt_s[k], t + 1)
                            pe.wait_ge(ev_s[k], t)
                            for c in range(2):
                                ins = pe.matmul(mma[k][:, 0:min(W, 2 * D)], xT[:, k, c * P:(c + 1) * P],
                                                w[:, c, 0:min(W, 2 * D)], start=(c == 0), stop=(c == 1))
                            if not first:
                                for c in range(2):
                                    ins = pe.matmul(mmb[k][:, 0:D], xT[:, k, c * P:(c + 1) * P],
                                                    w[:, c, 2 * D:W], start=(c == 0), stop=(c == 1))
                            ins.then_inc(mm_s[k], 1)

                        for k in range(2):
                            turn(0, k)
                        with pe.Fori(0, PAIRS) as t:
                            products(t, 0)
                            turn(t + 1, 0)
                            products(t, 1)
                            turn(t + 1, 1)
                end_phase()
        def registers(engine, row):
            return nc.values_load_multi_w_load_instructions(
                row, engines=[engine], min_val=0, max_val=NT - 1,
                skip_runtime_bounds_check_because="the table is clamped to NT - 1 and counts from 0")[1]

        def attend(l, queries):
            done = l * 16 * (NB // 2)
            LAST_N = NB + 1
            with ExitStack() as ph:
                kv = sb(ph, "kv", [P, 2 * UB, 2 * D])
                src_u = sb(ph, "src_u", [P, 2, UB], i32)
                ndrel_u = sb(ph, "ndrel_u", [P, 2, UB])
                drow = sb(ph, "drow", [P, 2, GB * P])
                resets = sb(ph, "resets", [P, RW], bf16)
                chain = sb(ph, "chain", [1, CW])
                far = sb(ph, "far", [P, 4 * P])
                hot_q = sb(ph, "hot_q", [P, 2, 4, P])
                hot_s = sb(ph, "hot_s", [P, 2, 4, P])
                prod = sb(ph, "prod", [P, 2, D])
                S = sb(ph, "S", [P, 2, 2 * H, UB])
                msg = sb(ph, "msg", [P, 2, 2, XW])
                sc = sb(ph, "sc", [P, 2, P])
                run_r = sb(ph, "run_r", [P, P])
                run_l = sb(ph, "run_l", [P, P])
                not_start = sb(ph, "not_start", [P, P], bf16)
                ex = sb(ph, "ex", [P, 2, P])
                W = sb(ph, "W", [P, 2, 2 * H, UB])
                left = sb(ph, "left", [1, 2, P + UB])
                right = sb(ph, "right", [1, P + 1])
                start = sb(ph, "start", [P, 2])
                carry = sb(ph, "carry", [P, 1])
                top = sb(ph, "top", [1, H])
                not_first = sb(ph, "not_first", [P, 3])
                unit_i = sb(ph, "unit_i", [P, 2], i32)
                unit_f = sb(ph, "unit_f", [P, 1])
                neg_p = sb(ph, "neg_p", [P, 1])
                delta = sb(ph, "delta", [1, H])
                scale = sb(ph, "scale", [P, H])
                qe = [ph.enter_context(nc.psum_tensor(f"qe{j}_{l}", [P, 2, 512], f32)) for j in range(2)]
                sum_p = [pb(ph, f"sum_p{j}") for j in range(2)]
                turned = pb(ph, "turned")
                small = pb(ph, "small")

                s = Names(pool)
                consts, dve_ready, pool_go = s.many(3)
                src_in, ndrel_in, drow_in = s.many(2), s.many(2), s.many(2)
                resets_in, chain_in = s.many(2)
                far_q_s, hot_q_s, far_s_s, hot_s_s = s.many(4)
                q_s, own_s, prod_s, red_s, msg_s, wcopy_s, sum_s, add_s = s.many(8)
                scT_s, sc_ready, not_start_s, chain_s, ends_s, cols_s = s.many(6)
                exp_s, wT_s, w_s, delta_s, scale_s, rescaled = s.many(6)
                CK = 15
                DVE_E, PE_E = mybir.EngineType.DVE, mybir.EngineType.PE

                def wait(eng, sem, v):
                    if not isinstance(v, int) or v > 0:
                        eng.wait_ge(sem, v)

                def periods(eng, period, first, last):
                    for n in range(first, 2):
                        period(n, n % 2, n // 2)
                    with eng.Fori(1, NB // 2 - 1) as t:
                        for b in range(2):
                            period(t * 2 + b, b, t)
                    for n in range(NB - 2, last + 1):
                        period(n, n % 2, n // 2)

                def message(n, g):
                    back, j = (2, g + 4) if g < 4 else (1, g - 4)
                    if isinstance(n, int) and not 0 <= n - back < NB:
                        return None
                    return back, j

                def has_scores(n):
                    return not isinstance(n, int) or n < NB

                def has_chain(n):
                    return not isinstance(n, int) or 1 <= n <= NB

                with nc.Block() as block:
                    @block.sync
                    def _(sp):
                        def load_src(n, par):
                            a = src_d[:, bass.ds(n * UB, UB)]
                            wait(sp, prod_s, n * GB - GB)
                            sp.dma_start(src_u[:, par, :], a).then_inc(src_in[par], 16)

                        def load_drow(n, f):
                            a = drel_d[bass.ds((n * UB + f * GB) * P, GB * P)].rearrange("(a n) -> a n", a=1).to_broadcast([P, GB * P])
                            wait(sp, far_q_s, n * 4 - 4 + 2 * f + 2)
                            sp.dma_start(drow[:, f, :], a).then_inc(drow_in[f], 16)

                        def period(n, par, t):
                            nxt = not isinstance(n, int) or n + 1 < NB
                            if nxt:
                                load_src(n + 1, 1 - par)
                                load_drow(n + 1, 0)
                            a = ndrel_d[:, bass.ds(n * UB, UB)]
                            wait(sp, far_s_s, n * 4 - 4)
                            sp.dma_start(ndrel_u[:, par, :], a).then_inc(ndrel_in[par], 16)
                            if nxt:
                                load_drow(n + 1, 1)
                            r, c = reset_d[bass.ds(n * P, P), :], chain_d[bass.ds(n, 1), :]
                            wait(sp, chain_s, n * CK)
                            wait(sp, not_start_s, n)
                            sp.dma_start(resets[:, :], r).then_inc(resets_in, 16)
                            wait(sp, scale_s, n)
                            sp.dma_start(chain[:, :], c).then_inc(chain_in, 16)

                        load_src(0, 0)
                        load_drow(0, 0)
                        load_drow(0, 1)
                        periods(sp, period, 0, NB - 1)
                        for sem, n in ((resets_in, NB), (chain_in, NB), (src_in[0], NB // 2), (src_in[1], NB // 2),
                                       (ndrel_in[0], NB // 2), (ndrel_in[1], NB // 2), (drow_in[0], NB), (drow_in[1], NB)):
                            sp.wait_ge(sem, 16 * n)

                    @block.gpsimd
                    def _(g):
                        g.iota(unit_i[:, 0:1], [[0, 1]], base=0, channel_multiplier=1).then_inc(consts, 1)

                        def period(n, par, t):
                            g.wait_ge(src_in[par], t * 16 + 16)
                            for j in range(GB):
                                wait(g, msg_s, n * GB - 2 * GB + j + 1)
                                g.sem_inc(pool_go, 1)
                                for u in (2 * j, 2 * j + 1):
                                    slot = par * UB + u
                                    g.indirect_dma_start(
                                        out=kv[:, slot, :], out_offset=None, in_=KVd,
                                        in_offset=bass.IndirectOffsetOnAxis(ap=src_u[:, par, u:u + 1], axis=0)
                                    ).then_inc(ring_in[slot], 16)

                        periods(g, period, 0, NB - 1)
                        for slot in range(2 * UB):
                            g.wait_ge(ring_in[slot], done + 16 * (NB // 2))

                    @block.scalar
                    def _(a):
                        a.wait_ge(dve_ready, 4)

                        def own_scores(n, par, g):
                            a.wait_ge(q_s, n * GB + g + 1)
                            wait(a, scT_s, n - 1)
                            a.activation(S[:, par, H:2 * H, 2 * g:2 * g + 2].rearrange("p h u -> p u h"),
                                         qe[g % 2][:, :, D:QW], ACT.Copy).then_inc(own_s, 1)

                        def hot_for_q(n, q, others):
                            f, c = q // 2, n * 4 + q
                            a.wait_ge(drow_in[f], n * 16 + 16)
                            wait(a, hot_q_s, c)
                            wait(a, hot_s_s, others)
                            a.activation(far[:, :], drow[:, f, (q % 2) * 4 * P:(q % 2 + 1) * 4 * P], ACT.Abs,
                                         bias=neg_p[:, 0:1]).then_inc(far_q_s, 1)
                            a.wait_ge(far_q_s, c + 1)
                            wait(a, q_s, c * 2 - 2)
                            a.activation(hot_q[:, q % 2, :, :].rearrange("p u e -> p (u e)"), far[:, :], ACT.Relu,
                                         bias=ones[:, 0:1], scale=-1.0).then_inc(hot_q_s, 1)

                        def hot_for_sums(m, par, loads, q, others):
                            c = m * 4 + q
                            a.wait_ge(ndrel_in[par], loads * 16)
                            wait(a, hot_s_s, c)
                            wait(a, hot_q_s, others)
                            for u in range(4):
                                ins = a.activation(far[:, u * P:(u + 1) * P], iota_f[:, :], ACT.Abs,
                                                   bias=ndrel_u[:, par, q * 4 + u:q * 4 + u + 1])
                            ins.then_inc(far_s_s, 1)
                            a.wait_ge(far_s_s, c + 1)
                            wait(a, sum_s, c * 2 - 2)
                            a.activation(hot_s[:, q % 2, :, :].rearrange("p u e -> p (u e)"), far[:, :], ACT.Relu,
                                         bias=ones[:, 0:1], scale=-1.0).then_inc(hot_s_s, 1)

                        def period(n, par, t):
                            for g in range(GB):
                                mj = message(n, g)
                                if mj:
                                    back, j = mj
                                    c = n * GB - back * GB + j
                                    a.wait_ge(w_s, n - back + 1)
                                    wait(a, sum_s, c - 1)
                                    a.activation(msg[:, g % 2, :, D:D + 2 * H],
                                                 W[:, (par + back) % 2, :, 2 * j:2 * j + 2].rearrange("p r u -> p u r"),
                                                 ACT.Copy).then_inc(wcopy_s, 1)
                                if g + 1 < GB and has_scores(n):
                                    own_scores(n, par, g + 1)
                                if g + 1 == GB and has_scores(n + 1):
                                    own_scores(n + 1, 1 - par, 0)
                                if g == 0 and has_chain(n):
                                    a.wait_ge(scT_s, n)
                                    wait(a, chain_s, n * CK - CK)
                                    a.activation(sc[:, :, :].rearrange("p r e -> p (r e)"), turned[:, 0:2 * P],
                                                 ACT.Copy).then_inc(sc_ready, 1)
                                    a.wait_ge(resets_in, n * 16)
                                    a.activation(not_start[:, :], resets[:, 0:P], ACT.Copy, bias=-BIG,
                                                 scale=-1.0).then_inc(not_start_s, 1)
                                if g == 3 and has_chain(n):
                                    a.wait_ge(chain_s, n * CK)
                                    flat = ex[:, :, :].rearrange("p r e -> p (r e)")
                                    a.activation(flat, flat, ACT.Exp).then_inc(exp_s, 1)
                                if g in (1, 3) and has_scores(n):
                                    hot_for_q(n, g // 2 + 2, n * 4 - 4 + g // 2)
                                elif g in (5, 7) and has_scores(n + 1):
                                    hot_for_q(n + 1, g // 2 - 2, n * 4 - 4 + g // 2)
                                elif g % 2 == 0 and message(n, 3 if g == 0 else 4):
                                    others = n * 4 + 2 + g // 2
                                    if isinstance(n, int):
                                        others = min(others, NB * 4)
                                    if g == 0:
                                        hot_for_sums(n - 2, par, t, 3, others)
                                    else:
                                        hot_for_sums(n - 1, 1 - par, t + par, g // 2 - 1, others)
                                if g == 3 and has_chain(n):
                                    a.wait_ge(delta_s, n)
                                    wait(a, rescaled, n * 2 - 2)
                                    a.activation(scale[:, :], small[:, 2 * P + H:2 * P + 2 * H], ACT.Exp).then_inc(scale_s, 1)
                                    a.wait_ge(wT_s, n)
                                    wait(a, msg_s, n * GB - 2 * GB)
                                    wait(a, wcopy_s, n * GB - 2 * GB)
                                    a.activation(W[:, 1 - par, :, :].rearrange("p r u -> p (r u)"), turned[:, 0:2 * P],
                                                 ACT.Copy).then_inc(w_s, 1)

                        hot_for_q(0, 0, 0)
                        hot_for_q(0, 1, 0)
                        own_scores(0, 0, 0)
                        periods(a, period, 0, LAST_N)

                    @block.vector
                    def _(v):
                        for b in range(2):
                            v.memset(msg[:, b, :, D + 2 * H:XW], 1.0)
                        v.memset(left[:, :, :], -BIG)
                        v.memset(right[:, :], -BIG)
                        v.memset(carry[:, :], -BIG).then_inc(dve_ready, 1)
                        v.wait_ge(consts, 1)
                        v.tensor_scalar(out=unit_i[:, 1:2], in0=unit_i[:, 0:1], scalar1=UB - 1, scalar2=None,
                                        op0=ALU.bitwise_and)
                        v.tensor_scalar(out=neg_p[:, :], in0=iota_p[:, :], scalar1=-1.0, scalar2=None,
                                        op0=ALU.mult).then_inc(dve_ready, 1)
                        v.wait_ge(dve_ready, 2)
                        v.tensor_copy(unit_f[:, :], unit_i[:, 1:2]).then_inc(dve_ready, 1)
                        v.wait_ge(dve_ready, 3)
                        v.tensor_scalar(out=not_first[:, 0:1], in0=unit_f[:, :], scalar1=0.0, scalar2=-BIG,
                                        op0=ALU.is_gt, op1=ALU.mult)
                        v.tensor_scalar(out=not_first[:, 1:2], in0=unit_f[:, :], scalar1=0.0, scalar2=-BIG,
                                        op0=ALU.is_equal, op1=ALU.mult)
                        v.tensor_scalar(out=not_first[:, 2:3], in0=unit_f[:, :], scalar1=float(UB - 1), scalar2=-BIG,
                                        op0=ALU.is_equal, op1=ALU.mult).then_inc(dve_ready, 1)
                        v.wait_ge(dve_ready, 4)

                        def heads(ap):
                            return ap.rearrange("p u (h d) -> p u h d", d=DH)

                        def products(n, par, t, g):
                            for u in (2 * g, 2 * g + 1):
                                v.wait_ge(ring_in[par * UB + u], t * 16 + done + 16)
                            v.wait_ge(own_s, n * GB + g + 1)
                            wait(v, red_s, n * GB + g)
                            v.tensor_tensor(out=prod[:, :, :], in0=qe[g % 2][:, :, 0:D],
                                            in1=kv[:, par * UB + 2 * g:par * UB + 2 * g + 2, 0:D],
                                            op=ALU.mult).then_inc(prod_s, 1)

                        def scores(n, par, g):
                            v.wait_ge(prod_s, n * GB + g + 1)
                            wait(v, scT_s, n - 1)
                            v.tensor_reduce(out=S[:, par, 0:H, 2 * g:2 * g + 2].rearrange("p h u -> p u h"),
                                            in_=heads(prod[:, :, :]), axis=AX.X, op=ALU.add).then_inc(red_s, 1)

                        def messages(n, par, g, back, j):
                            c = n * GB - back * GB + j
                            m_par = (par + back) % 2
                            v.wait_ge(w_s, n - back + 1)
                            wait(v, sum_s, c - 1)
                            v.tensor_tensor(out=heads(msg[:, g % 2, :, 0:D]),
                                            in0=heads(kv[:, m_par * UB + 2 * j:m_par * UB + 2 * j + 2, D:2 * D]),
                                            in1=W[:, m_par, 0:H, 2 * j:2 * j + 2].rearrange("p r u -> p u r")
                                            .unsqueeze(3).to_broadcast([P, 2, H, DH]), op=ALU.mult).then_inc(msg_s, 1)

                        def add(c, g, tile):
                            v.wait_ge(sum_s, c + 1)
                            wait(v, add_s, c)
                            at = sums[:, bass.ds(tile * XW, XW)]
                            v.tensor_tensor(out=at, in0=at, in1=sum_p[g][:, 0:XW], op=ALU.add).then_inc(add_s, 1)

                        def step(i, k):
                            return i * CK - CK + k

                        def chain_units(n):
                            v.wait_ge(sc_ready, n)
                            v.tensor_tensor(out=run_r[:, :], in0=sc[:, 0, :], in1=sc[:, 1, :], op=ALU.max).then_inc(chain_s, 1)
                            v.wait_ge(resets_in, n * 16)
                            v.wait_ge(chain_s, step(n, 1))
                            v.tensor_tensor_scan(run_l[:, :], resets[:, 0:P], run_r[:, :], carry[:, 0:1], ALU.add, ALU.max
                                                 ).then_inc(chain_s, 1)
                            v.wait_ge(chain_s, step(n, 2))
                            v.tensor_tensor_scan(run_r[:, ::-1], resets[:, 1:RW][:, ::-1], run_r[:, ::-1], -BIG, ALU.add, ALU.max
                                                 ).then_inc(chain_s, 1)

                        def chain_rows(n, par):
                            v.wait_ge(ends_s, n)
                            v.wait_ge(chain_in, n * 16)
                            v.tensor_tensor_scan(left[0:1, par, 1:P + 1], chain[0:1, 0:P], small[0:1, 0:P], -BIG,
                                                 ALU.add, ALU.max).then_inc(chain_s, 1)
                            v.tensor_tensor_scan(right[0:1, 0:P][:, ::-1], chain[0:1, P:2 * P][:, ::-1],
                                                 small[0:1, P:2 * P][:, ::-1], -BIG, ALU.add, ALU.max).then_inc(chain_s, 1)
                            v.wait_ge(not_start_s, n)
                            v.tensor_tensor(out=sc[:, 1, :], in0=sc[:, 1, :], in1=not_start[:, :],
                                            op=ALU.add).then_inc(chain_s, 1)
                            old = left[0:1, 1 - par, UB:P + 1:UB]
                            v.wait_ge(chain_s, step(n, 5))
                            v.tensor_tensor(out=top[:, :], in0=old, in1=right[0:1, 0:P:UB], op=ALU.max).then_inc(chain_s, 1)
                            v.wait_ge(chain_s, step(n, 7))
                            v.tensor_tensor(out=delta[:, :], in0=old, in1=top[:, :], op=ALU.subtract).then_inc(chain_s, 1)

                        def chain_edges(n):
                            v.wait_ge(cols_s, n)
                            v.tensor_tensor(out=start[:, 0:1], in0=small[:, 2 * P:2 * P + 1], in1=not_first[:, 1:2],
                                            op=ALU.add).then_inc(chain_s, 1)
                            v.tensor_tensor(out=start[:, 1:2], in0=small[:, 2 * P + 1:2 * P + 2], in1=not_first[:, 2:3],
                                            op=ALU.add).then_inc(chain_s, 1)
                            v.tensor_tensor(out=carry[:, :], in0=small[:, 2 * P + 2:2 * P + 3], in1=not_first[:, 0:1],
                                            op=ALU.add).then_inc(chain_s, 1)
                            v.wait_ge(chain_s, step(n, 9))
                            v.tensor_tensor_scan(run_l[:, :], resets[:, 0:P], run_l[:, :], start[:, 0:1], ALU.add, ALU.max
                                                 ).then_inc(chain_s, 1)
                            v.wait_ge(chain_s, step(n, 10))
                            v.tensor_tensor_scan(run_r[:, ::-1], resets[:, 1:RW][:, ::-1], run_r[:, ::-1], start[:, 1:2],
                                                 ALU.add, ALU.max).then_inc(chain_s, 1)
                            v.wait_ge(chain_s, step(n, 13))
                            v.tensor_tensor(out=run_l[:, :], in0=run_l[:, :], in1=run_r[:, :], op=ALU.max).then_inc(chain_s, 1)
                            wait(v, wT_s, n - 1)
                            v.wait_ge(chain_s, step(n, 14))
                            v.tensor_tensor(out=ex[:, :, :], in0=sc[:, :, :],
                                            in1=run_l[:, :].unsqueeze(1).to_broadcast([P, 2, P]),
                                            op=ALU.subtract).then_inc(chain_s, 1)

                        def period(n, par, t):
                            fixed = isinstance(n, int)
                            lo = n * GB - GB - 5
                            if not fixed:
                                tiles = registers(DVE_E, nt_row[0:1, bass.ds(lo, GB)])
                            elif n == 0:
                                tiles = ()
                            else:
                                a, b = max(lo, 0), min(lo + GB, NG)
                                tiles = [None] * (a - lo) + list(registers(DVE_E, nt_row[0:1, a:b]))
                            b_par = 1 - par
                            for g in range(GB):
                                if has_chain(n):
                                    if g == 1:
                                        chain_units(n)
                                    elif g == 2:
                                        chain_rows(n, b_par)
                                    elif g == 3:
                                        chain_edges(n)
                                if has_scores(n):
                                    products(n, par, t, g)
                                mj = message(n, g)
                                if mj and g != 4:
                                    messages(n, par, g, *mj)
                                if has_scores(n):
                                    scores(n, par, g)
                                before = message(n, g - 1) if g else message(n - 1, GB - 1)
                                if before:
                                    if g == 5 and has_chain(n):
                                        v.wait_ge(rescaled, n * 2)
                                    add(lo + g, (g - 1) % 2, tiles[g])
                                if has_chain(n):
                                    if g == 4:
                                        first = tiles[5] * XW
                                        v.wait_ge(scale_s, n)
                                        wait(v, add_s, n * GB - GB)
                                        at = sums[:, bass.ds(first, D)].rearrange("p (h d) -> p h d", d=DH)
                                        v.tensor_tensor(out=at, in0=at, in1=scale[:, :].unsqueeze(2).to_broadcast([P, H, DH]),
                                                        op=ALU.mult).then_inc(rescaled, 1)
                                        at = sums[:, bass.ds(first + D, 2 * H)].rearrange("p (r h) -> p r h", h=H)
                                        v.tensor_tensor(out=at, in0=at, in1=scale[:, :].unsqueeze(1).to_broadcast([P, 2, H]),
                                                        op=ALU.mult).then_inc(rescaled, 1)
                                if mj and g == 4:
                                    messages(n, par, g, *mj)

                        periods(v, period, 0, LAST_N)

                    @block.tensor
                    def _(pe):
                        def spread(n, par, g, tile):
                            q, c = g // 2, n * GB + g
                            pe.wait_ge(hot_q_s, n * 4 + q + 1)
                            wait(pe, prod_s, c - 1)
                            for u in range(2):
                                ins = pe.matmul(qe[g % 2][:, u, 0:QW], hot_q[:, q % 2, (2 * g + u) % 4, :],
                                                queries[:, bass.ds(tile * QW, QW)], start=True, stop=True)
                            ins.then_inc(q_s, 1)

                        def sum_up(n, g, back, j):
                            c = n * GB - back * GB + j
                            pe.wait_ge(hot_s_s, n * 4 - back * 4 + j // 2 + 1)
                            pe.wait_ge(wcopy_s, c + 1)
                            wait(pe, add_s, c - 1)
                            pe.wait_ge(msg_s, c + 1)
                            for u in range(2):
                                ins = pe.matmul(sum_p[g % 2][:, 0:XW], hot_s[:, (j // 2) % 2, (2 * j + u) % 4, :],
                                                msg[:, g % 2, u, :], start=(u == 0), stop=(u == 1))
                            ins.then_inc(sum_s, 1)

                        def period(n, par, t):
                            if not isinstance(n, int):
                                tiles = registers(PE_E, nt_row[0:1, bass.ds(n * GB + 1, GB)])
                            elif n < NB:
                                tiles = registers(PE_E, nt_row[0:1, n * GB + 1:min(n * GB + 1 + GB, NG)])
                            for g in range(GB):
                                if g + 1 < GB and has_scores(n):
                                    spread(n, par, g + 1, tiles[g])
                                if g + 1 == GB and has_scores(n + 1):
                                    spread(n + 1, 1 - par, 0, tiles[g])
                                if has_chain(n):
                                    if g == 0:
                                        pe.wait_ge(red_s, n * GB)
                                        pe.wait_ge(own_s, n * GB)
                                        wait(pe, w_s, n - 1)
                                        for r in range(2):
                                            ins = pe.transpose(turned[:, r * P:(r + 1) * P],
                                                               S[:, 1 - par, r * H:(r + 1) * H, :].rearrange("p h u -> p (h u)"),
                                                               ident[:, :])
                                        ins.then_inc(scT_s, 1)
                                    elif g == 1:
                                        pe.wait_ge(chain_s, n * CK - CK + 3)
                                        wait(pe, scale_s, n - 1)
                                        pe.transpose(small[0:1, 0:P], run_l[:, P - 1:P], ident[:, :])
                                        pe.transpose(small[0:1, P:2 * P], run_r[:, 0:1], ident[:, :]).then_inc(ends_s, 1)
                                    elif g == 2:
                                        pe.wait_ge(chain_s, n * CK - CK + 5)
                                        for i, row in enumerate((left[0:1, 1 - par, 0:P], right[0:1, 1:P + 1],
                                                                 left[0:1, 1 - par, UB:UB + P])):
                                            ins = pe.matmul(small[:, 2 * P + i:2 * P + i + 1], row, ones[0:1, 0:1],
                                                            start=True, stop=True)
                                        ins.then_inc(cols_s, 1)
                                    elif g == 3:
                                        pe.wait_ge(chain_s, n * CK - CK + 11)
                                        pe.matmul(small[:, 2 * P + H:2 * P + 2 * H], chain[0:1, 2 * P:3 * P], delta[0:1, :],
                                                  start=True, stop=True).then_inc(delta_s, 1)
                                mj = message(n, g)
                                if mj:
                                    sum_up(n, g, *mj)
                                if g == 3 and has_chain(n):
                                    pe.wait_ge(exp_s, n)
                                    pe.transpose(turned[:, 0:P], ex[:, 0, :], ident[:, :])
                                    pe.transpose(turned[:, P:2 * P], ex[:, 1, :], ident[:, :]).then_inc(wT_s, 1)

                        pe.wait_ge(consts, 1)
                        pe.wait_ge(dve_ready, 4)
                        first, = registers(PE_E, nt_row[0:1, 0:1])
                        spread(0, 0, 0, first)
                        periods(pe, period, 0, LAST_N)
                end_phase()
        def update(l):
            FB = FF // P
            with ExitStack() as ph:
                wo_s = sb(ph, "wo_s", [P, 2, D])
                w1_s = sb(ph, "w1_s", [P, 2, FF])
                w2_s = sb(ph, "w2_s", [P, FB, D])
                bo_b = sb(ph, "bo_b", [P, D])
                b2_b = sb(ph, "b2_b", [P, D])
                b1_c = sb(ph, "b1_c", [P, FB])
                gcol = sb(ph, "gcol", [P, 2])
                bcol = sb(ph, "bcol", [P, 2])
                hin = sb(ph, "hin", [P, 2, D])
                vin = sb(ph, "vin", [P, 2, D])
                hb = sb(ph, "hb", [P, 2, D])
                h1 = sb(ph, "h1", [P, 2, D])
                h1b = sb(ph, "h1b", [P, 2, D])
                res = sb(ph, "res", [P, 2, D])
                zt = sb(ph, "zt", [P, 2, 3, H])
                own = sb(ph, "own", [P, 2, D])
                agg = sb(ph, "agg", [P, 2, D])
                att = sb(ph, "att", [P, 2, D])
                st = sb(ph, "st", [P, 2, 6])
                mv = sb(ph, "mv", [P, 2, 2])
                veps = sb(ph, "veps", [P, 2, 1])
                rs = sb(ph, "rs", [P, 2, 1])
                xn = sb(ph, "xn", [P, 2, D])
                aT = sb(ph, "aT", [P, 2, D])
                xT = sb(ph, "xT", [P, 2, D])
                uT = sb(ph, "uT", [P, 2, FB, P])
                ea = sb(ph, "ea", [P, 2, EG, YW])
                srow = sb(ph, "srow", [P, 2, EG * P], i32)
                scol = sb(ph, "scol", [P, 2, EG], i32)
                scol_f = sb(ph, "scol_f", [P, 2, EG])
                same = sb(ph, "same", [P, 2, EG, P])
                before = sb(ph, "before", [P, EG, P])
                count = sb(ph, "count", [P, 2, EG])
                away = sb(ph, "away", [P, 2, 2, EG])
                dest = sb(ph, "dest", [P, 2, EG], i32)
                dummy = sb(ph, "dummy", [P, 1])
                tril = sb(ph, "tril", [P, P])
                ysum = sb(ph, "ysum", [P, 2, EG, YW])
                tp = [pb(ph, f"tp{k}") for k in range(2)]
                wo_p, w2_p = pb(ph, "wo_p"), pb(ph, "w2_p")
                w1_p = [pb(ph, f"w1_p{f}") for f in range(2)]
                y_p = [pb(ph, f"y_p{b}") for b in range(2)]
                PARTS = ((0, 0, 3), (1, 3, 6), (0, 6, EG))
                s = Names(pool)
                w_in_s, prep, bmm, const_s, pool_go, join, s3_c, aggr_go, tril_s = s.many(9)
                hv_in, e_in, n_c, hb_s, ta_s, at_s, wo_d, h1_s, st_s, mv_s, ve_s, rs_s = (s.many(2) for _ in range(12))
                h1b_s, xn_s, tx_s, xt_s, w1_d, gel, w2_d, out_s, stored, y_d, y_ev, idx_s = (s.many(2) for _ in range(12))
                sc0 = l * 32 * PAIRS
                S3N = EG + 5

                with nc.Block() as block:
                    @block.sync
                    def _(sp):
                        slow = dict(allow_slow_non_contiguous=True)
                        sp.dma_start(wo_s[:, :, :], wo[l].rearrange("(c p) n -> p c n", p=P)).then_inc(w_in_s, 16)
                        sp.dma_start(w1_s[:, :, :], w1[l].rearrange("(c p) n -> p c n", p=P)).then_inc(w_in_s, 16)
                        sp.dma_start(w2_s[:, :, :], w2[l].rearrange("(c p) n -> p c n", p=P)).then_inc(w_in_s, 16)
                        sp.dma_start(bo_b[:, :], bo[l:l + 1, :].to_broadcast([P, D])).then_inc(w_in_s, 16)
                        sp.dma_start(b2_b[:, :], b2[l:l + 1, :].to_broadcast([P, D])).then_inc(w_in_s, 16)
                        sp.dma_start(b1_c[:, :], b1[l].rearrange("(c p) -> p c", p=P), **slow).then_inc(w_in_s, 16)
                        sp.dma_start(gcol[:, :], ln2_g[l].rearrange("(c p) -> p c", p=P), **slow).then_inc(w_in_s, 16)
                        sp.dma_start(bcol[:, :], ln2_b[l].rearrange("(c p) -> p c", p=P), **slow).then_inc(w_in_s, 16)
                        sp.wait_ge(const_s, 1)

                        def load_nodes(t, k):
                            sp.dma_start(hin[:, k, :], rows(Hd, t * 2 + k)).then_inc(hv_in[k], 16)
                            sp.dma_start(vin[:, k, :], rows(KVd, t * 2 + k)[:, D:2 * D]).then_inc(hv_in[k], 16)

                        def load_edges(t, k):
                            g = l * NT + t * 2 + k
                            sp.dma_start(ea[:, k, :, 0:ED],
                                         edge_attr[bass.ds(g * P, P), :].rearrange("p (j w) -> p j w", w=ED)).then_inc(e_in[k], 16)
                            sp.dma_start(srow[:, k, :], src_rows[bass.ds(g, 1), :].to_broadcast([P, EG * P])).then_inc(e_in[k], 16)
                            sp.dma_start(scol[:, k, :], src_cols[bass.ds(g * P, P), :]).then_inc(e_in[k], 16)

                        for k in range(2):
                            load_nodes(0, k)
                            load_edges(0, k)
                        for k in range(2):
                            sp.wait_ge(hb_s[k], 1)
                            sp.wait_ge(n_c[k], 6)
                            load_nodes(1, k)
                        with sp.Fori(0, PAIRS) as t:
                            for k in range(2):
                                sp.wait_ge(hb_s[k], t + 2)
                                sp.wait_ge(n_c[k], t * 6 + 12)
                                load_nodes(t + 2, k)
                            for k in range(2):
                                sp.wait_ge(out_s[k], t + 1)
                                sp.dma_start(rows(Hd, t * 2 + k), res[:, k, :]).then_inc(stored[k], 16)
                                sp.wait_ge(y_ev[0], t * 4 + k * 2 + 2)
                                load_edges(t + 1, k)
                        for k in range(2):
                            sp.wait_ge(stored[k], 16 * PAIRS)
                            sp.wait_ge(hv_in[k], 32 * (PAIRS + 2))
                            sp.wait_ge(e_in[k], 48 * (PAIRS + 1))

                    @block.gpsimd
                    def _(g):
                        g.memset(tril[:, :], 1.0).then_inc(tril_s, 1)
                        g.wait_ge(tril_s, 1)
                        g.affine_select(out=tril[:, :], in_=tril[:, :], compare_op=ALU.is_gt, fill=0.0,
                                        base=0, pattern=[[-1, P]], channel_multiplier=1).then_inc(tril_s, 1)
                        g.wait_ge(w_in_s, 16 * 8)

                        def add_bo(t, k):
                            g.wait_ge(hv_in[k], t * 32 + 32)
                            g.wait_ge(h1_s[k], t)
                            g.tensor_tensor(out=hb[:, k, :], in0=hin[:, k, :], in1=bo_b[:, :], op=ALU.add).then_inc(hb_s[k], 1)

                        def scale(t, k):
                            g.wait_ge(ve_s[k], t + 1)
                            g.tensor_tensor(out=rs[:, k, :], in0=veps[:, k, :], in1=neghalf[:, :], op=ALU.pow).then_inc(rs_s[k], 1)
                            g.wait_ge(out_s[k], t)
                            g.tensor_tensor(out=h1b[:, k, :], in0=h1[:, k, :], in1=b2_b[:, :], op=ALU.add).then_inc(h1b_s[k], 1)

                        def scatter(t, k):
                            g.wait_ge(idx_s[k], t + 1)
                            for b, j0, j1 in PARTS:
                                if b == 0:
                                    g.wait_ge(y_ev[0], t * 4 + k * 2 + (1 if j0 == 0 else 2))
                                else:
                                    g.wait_ge(y_ev[1], t * 2 + k + 1)
                                for j in range(j0, j1):
                                    r = j % TABLES
                                    if j >= TABLES:
                                        g.wait_ge(sc_s[k][r], t * 32 + sc0 + 16)
                                    elif k == 0:
                                        g.wait_ge(sc_s[1][r], t * 32 + sc0)
                                    else:
                                        g.wait_ge(sc_s[0][r], t * 32 + sc0 + 32)
                                    g.sem_inc(pool_go, 1)
                                    g.indirect_dma_start(
                                        out=sum_d[r], out_offset=bass.IndirectOffsetOnAxis(ap=dest[:, k, j:j + 1], axis=0),
                                        in_=ysum[:, k, j, :], in_offset=None, compute_op=ALU.add).then_inc(sc_s[k][r], 16)

                        for k in range(2):
                            add_bo(0, k)
                        for k in range(2):
                            scale(0, k)
                        with g.Fori(0, PAIRS) as t:
                            for k in range(2):
                                add_bo(t + 1, k)
                            for k in range(2):
                                scale(t + 1, k)
                                scatter(t, k)
                        for k in range(2):
                            for r in range(TABLES):
                                g.wait_ge(sc_s[k][r], sc0 + 32 * PAIRS)

                    @block.vector
                    def _(v):
                        for k in range(2):
                            ins = v.memset(ea[:, k, :, ED:YW], 1.0)
                        ins.then_inc(const_s, 1)
                        v.tensor_scalar(out=dummy[:, :], in0=iota_p[:, :], scalar1=float(DUMMY), scalar2=None,
                                        op0=ALU.add).then_inc(join, 1)
                        v.wait_ge(w_in_s, 16 * 8)
                        v.wait_ge(bmm, 1)
                        v.tensor_tensor(out=b1_c[:, :], in0=b1_c[:, :], in1=w2_p[:, 0:FB], op=ALU.add)
                        for c in range(2):
                            ins = v.tensor_scalar(out=w1_s[:, c, :], in0=w1_s[:, c, :], scalar1=gcol[:, c:c + 1],
                                                  scalar2=None, op0=ALU.mult)
                        ins.then_inc(prep, 1)
                        v.wait_ge(join, 1)
                        v.wait_ge(tril_s, 2)

                        def heads(ap):
                            return ap.rearrange("p (h d) -> p h d", d=DH)

                        def attention(t, k):
                            at = 0 if isinstance(t, int) and t == PAIRS else (t * 2 + k) * XW
                            v.wait_ge(ta_s[k], t)
                            v.tensor_tensor(out=zt[:, k, 0, :], in0=sums[:, bass.ds(at + D, H)],
                                            in1=sums[:, bass.ds(at + D + H, H)], op=ALU.add).then_inc(n_c[k], 1)
                            v.wait_ge(hv_in[k], t * 32 + 32)
                            v.tensor_tensor(out=heads(own[:, k, :]), in0=heads(vin[:, k, :]),
                                            in1=sums[:, bass.ds(at + D + H, H)].unsqueeze(2).to_broadcast([P, H, DH]),
                                            op=ALU.mult).then_inc(n_c[k], 1)
                            v.wait_ge(n_c[k], t * 6 + 1)
                            v.scalar_tensor_tensor(out=zt[:, k, 1, :], in0=zt[:, k, 0, :], scalar=0.0, in1=zt[:, k, 0, :],
                                                   op0=ALU.is_equal, op1=ALU.add).then_inc(n_c[k], 1)
                            v.wait_ge(n_c[k], t * 6 + 2)
                            v.tensor_tensor(out=agg[:, k, :], in0=own[:, k, :], in1=sums[:, bass.ds(at, D)],
                                            op=ALU.add).then_inc(n_c[k], 1)
                            v.wait_ge(n_c[k], t * 6 + 3)
                            v.reciprocal(zt[:, k, 2, :], zt[:, k, 1, :]).then_inc(n_c[k], 1)
                            v.wait_ge(n_c[k], t * 6 + 5)
                            v.tensor_tensor(out=heads(att[:, k, :]), in0=heads(agg[:, k, :]),
                                            in1=zt[:, k, 2, :].unsqueeze(2).to_broadcast([P, H, DH]),
                                            op=ALU.mult).then_inc(n_c[k], 1)

                        def stats(t, k):
                            v.wait_ge(wo_d[k], t + 1)
                            v.wait_ge(hb_s[k], t + 1)
                            v.wait_ge(h1b_s[k], t)
                            v.tensor_tensor(out=h1[:, k, :], in0=wo_p[:, k * D:(k + 1) * D], in1=hb[:, k, :],
                                            op=ALU.add).then_inc(h1_s[k], 1)
                            v.wait_ge(h1_s[k], t + 1)
                            v.bn_stats(out=st[:, k, :], in_=h1[:, k, :]).then_inc(st_s[k], 1)
                            v.wait_ge(st_s[k], t + 1)
                            v.sem_inc(aggr_go, 1)
                            v.bn_aggr(out=mv[:, k, :], in_=st[:, k, :]).then_inc(mv_s[k], 1)
                            v.wait_ge(mv_s[k], t + 1)
                            v.tensor_scalar(out=veps[:, k, :], in0=mv[:, k, 1:2], scalar1=EPS, scalar2=None,
                                            op0=ALU.add).then_inc(ve_s[k], 1)

                        def norm(t, k):
                            v.wait_ge(rs_s[k], t + 1)
                            v.wait_ge(tx_s[k], t)
                            v.tensor_scalar(out=xn[:, k, :], in0=h1[:, k, :], scalar1=mv[:, k, 0:1],
                                            scalar2=rs[:, k, :], op0=ALU.subtract, op1=ALU.mult).then_inc(xn_s[k], 1)

                        def result(t, k):
                            v.wait_ge(w2_d[k], t + 1)
                            v.wait_ge(h1b_s[k], t + 1)
                            v.wait_ge(stored[k], t * 16)
                            v.tensor_tensor(out=res[:, k, :], in0=w2_p[:, k * D:(k + 1) * D], in1=h1b[:, k, :],
                                            op=ALU.add).then_inc(out_s[k], 1)

                        def repeats(t, k):
                            at = (t * 2 + k) * S3N
                            v.wait_ge(e_in[k], t * 48 + 48)
                            v.tensor_copy(scol_f[:, k, :], scol[:, k, :]).then_inc(s3_c, 1)
                            v.wait_ge(s3_c, at + 1)
                            for j in range(EG):
                                ins = v.tensor_scalar(out=same[:, k, j, :], in0=srow[:, k, j * P:(j + 1) * P],
                                                      scalar1=scol_f[:, k, j:j + 1], scalar2=None, op0=ALU.is_equal)
                            ins.then_inc(s3_c, 1)
                            v.wait_ge(s3_c, at + 2)
                            for j in range(EG):
                                v.tensor_tensor_reduce(out=before[:, j, :], in0=same[:, k, j, :], in1=tril[:, :], scale=1.0,
                                                       scalar=0.0, op0=ALU.mult, op1=ALU.add,
                                                       accum_out=count[:, k, j:j + 1]).then_inc(s3_c, 1)
                            v.tensor_scalar(out=away[:, k, 0, :], in0=scol_f[:, k, :], scalar1=-1.0, scalar2=dummy[:, 0:1],
                                            op0=ALU.mult, op1=ALU.add).then_inc(s3_c, 1)
                            v.wait_ge(s3_c, at + EG + 3)
                            v.scalar_tensor_tensor(out=away[:, k, 1, :], in0=count[:, k, :], scalar=0.0, in1=away[:, k, 0, :],
                                                   op0=ALU.is_gt, op1=ALU.mult).then_inc(s3_c, 1)
                            v.wait_ge(s3_c, at + EG + 4)
                            for r in range(TABLES):
                                v.wait_ge(sc_s[k][r], t * 32 + sc0)
                            v.tensor_tensor(out=dest[:, k, :], in0=away[:, k, 1, :], in1=scol_f[:, k, :],
                                            op=ALU.add).then_inc(idx_s[k], 1)
                            v.wait_ge(idx_s[k], t + 1)
                            v.sem_inc(s3_c, 1)

                        for k in range(2):
                            attention(0, k)
                        for k in range(2):
                            stats(0, k)
                        for k in range(2):
                            norm(0, k)

                        def turn(t):
                            attention(t + 1, 0)
                            repeats(t, 0)
                            result(t, 0)
                            stats(t + 1, 0)
                            attention(t + 1, 1)
                            norm(t + 1, 0)
                            repeats(t, 1)
                            result(t, 1)
                            stats(t + 1, 1)
                            norm(t + 1, 1)

                        with v.Fori(0, PAIRS - 1) as t:
                            turn(t)
                        turn(PAIRS - 1)

                    @block.scalar
                    def _(a):
                        def turned_att(t, k):
                            a.wait_ge(ta_s[k], t + 1)
                            a.wait_ge(wo_d[k], t)
                            a.activation(aT[:, k, :], tp[k][:, 0:D], ACT.Copy).then_inc(at_s[k], 1)

                        def turned_norm(t, k):
                            a.wait_ge(tx_s[k], t + 1)
                            a.wait_ge(w1_d[k], t * 2)
                            a.activation(xT[:, k, :], tp[k][:, D:2 * D], ACT.Copy).then_inc(xt_s[k], 1)

                        def gelu(t, k):
                            a.wait_ge(w2_d[k], t)
                            for f in range(2):
                                a.wait_ge(w1_d[k], t * 2 + f + 1)
                                for b in range(4):
                                    j = f * 4 + b
                                    ins = a.activation(uT[:, k, j, :], w1_p[f][:, b * P:(b + 1) * P], ACT.Gelu,
                                                       bias=b1_c[:, j:j + 1])
                                ins.then_inc(gel[f], 1)

                        def sums_out(t, k):
                            for r in range(TABLES):
                                a.wait_ge(sc_s[k][r], t * 32 + sc0)
                            for b, j0, j1 in PARTS:
                                if b == 0:
                                    a.wait_ge(y_d[0], t * 4 + k * 2 + (1 if j0 == 0 else 2))
                                else:
                                    a.wait_ge(y_d[1], t * 2 + k + 1)
                                a.activation(ysum[:, k, j0:j1, :].rearrange("p j w -> p (j w)"),
                                             y_p[b][:, 0:(j1 - j0) * YW], ACT.Copy).then_inc(y_ev[b], 1)

                        for k in range(2):
                            turned_att(0, k)
                        for k in range(2):
                            turned_norm(0, k)
                        a.wait_ge(prep, 1)
                        with a.Fori(0, PAIRS) as t:
                            gelu(t, 0)
                            turned_att(t + 1, 0)
                            sums_out(t, 0)
                            gelu(t, 1)
                            turned_att(t + 1, 1)
                            turned_norm(t + 1, 0)
                            sums_out(t, 1)
                            turned_norm(t + 1, 1)

                    @block.tensor
                    def _(pe):
                        pe.wait_ge(w_in_s, 16 * 8)
                        for j in range(FB):
                            for c in range(2):
                                ins = pe.matmul(w2_p[:, j:j + 1], w1_s[:, c, j * P:(j + 1) * P], bcol[:, c:c + 1],
                                                start=(c == 0), stop=(c == 1))
                        ins.then_inc(bmm, 1)
                        pe.wait_ge(prep, 1)

                        def turn_att(t, k):
                            pe.wait_ge(n_c[k], t * 6 + 6)
                            pe.wait_ge(xt_s[k], t)
                            for c in range(2):
                                ins = pe.transpose(tp[k][:, c * P:(c + 1) * P], att[:, k, c * P:(c + 1) * P], ident[:, :])
                            ins.then_inc(ta_s[k], 1)

                        def out_proj(t, k):
                            pe.wait_ge(at_s[k], t + 1)
                            pe.wait_ge(h1_s[1 - k], t + k)
                            for c in range(2):
                                ins = pe.matmul(wo_p[:, k * D:(k + 1) * D], aT[:, k, c * P:(c + 1) * P], wo_s[:, c, :],
                                                start=(c == 0), stop=(c == 1))
                            ins.then_inc(wo_d[k], 1)

                        def turn_norm(t, k):
                            pe.wait_ge(xn_s[k], t + 1)
                            pe.wait_ge(at_s[k], t + 1)
                            for c in range(2):
                                ins = pe.transpose(tp[k][:, D + c * P:D + (c + 1) * P], xn[:, k, c * P:(c + 1) * P], ident[:, :])
                            ins.then_inc(tx_s[k], 1)

                        def up(t, k):
                            pe.wait_ge(xt_s[k], t + 1)
                            for f in range(2):
                                pe.wait_ge(gel[f], t * 2 + k)
                                for b in range(4):
                                    j = f * 4 + b
                                    for c in range(2):
                                        ins = pe.matmul(w1_p[f][:, b * P:(b + 1) * P], w1_s[:, c, j * P:(j + 1) * P],
                                                        xT[:, k, c * P:(c + 1) * P], start=(c == 0), stop=(c == 1))
                                ins.then_inc(w1_d[k], 1)

                        def down(t, k):
                            pe.wait_ge(out_s[1 - k], t + k)
                            for f in range(2):
                                pe.wait_ge(gel[f], t * 2 + k + 1)
                                for b in range(4):
                                    j = f * 4 + b
                                    ins = pe.matmul(w2_p[:, k * D:(k + 1) * D], uT[:, k, j, :], w2_s[:, j, :],
                                                    start=(j == 0), stop=(j == FB - 1))
                            ins.then_inc(w2_d[k], 1)

                        def sum_group(t, k):
                            pe.wait_ge(e_in[k], t * 48 + 48)
                            pe.wait_ge(s3_c, (t * 2 + k) * S3N + 2)
                            for b, j0, j1 in PARTS:
                                if b == 0:
                                    pe.wait_ge(y_ev[0], t * 4 + k * 2 + (0 if j0 == 0 else 1))
                                else:
                                    pe.wait_ge(y_ev[1], t * 2 + k)
                                for j in range(j0, j1):
                                    ins = pe.matmul(y_p[b][:, (j - j0) * YW:(j - j0 + 1) * YW], same[:, k, j, :],
                                                    ea[:, k, j, :], start=True, stop=True)
                                ins.then_inc(y_d[b], 1)

                        for k in range(2):
                            turn_att(0, k)
                        for k in range(2):
                            out_proj(0, k)
                        for k in range(2):
                            turn_norm(0, k)
                        with pe.Fori(0, PAIRS) as t:
                            up(t, 0)
                            turn_att(t + 1, 0)
                            down(t, 0)
                            out_proj(t + 1, 0)
                            sum_group(t, 0)
                            up(t, 1)
                            turn_att(t + 1, 1)
                            turn_norm(t + 1, 0)
                            down(t, 1)
                            out_proj(t + 1, 1)
                            sum_group(t, 1)
                            turn_norm(t + 1, 1)
                end_phase()

        def finish():
            with ExitStack() as ph:
                wsum_s = sb(ph, "wsum_s", [P, D])
                bsum_b = sb(ph, "bsum_b", [P, D])
                wb = sb(ph, "wb", [2, 2, D])
                vecs = sb(ph, "vecs", [2, 2, 2, P])
                xin = sb(ph, "xin", [P, 2, D])
                hin = sb(ph, "hin", [P, 2, D])
                sin = sb(ph, "sin", [P, 2, TABLES, YW])
                x1 = sb(ph, "x1", [P, 2, D])
                pair = sb(ph, "pair", [P, 2, 2, YW])
                tot = sb(ph, "tot", [P, 2, YW])
                totT = sb(ph, "totT", [P, 2, P])
                ideg = sb(ph, "ideg", [P, 2, 2], i32)
                zi = sb(ph, "zi", [P, 2, D])
                zo = sb(ph, "zo", [P, 2, D])
                sg = sb(ph, "sg", [P, 2, 2 * D])
                st = sb(ph, "st", [P, 2, 6])
                mv = sb(ph, "mv", [P, 2, 2])
                veps = sb(ph, "veps", [P, 2, 1])
                rs = sb(ph, "rs", [P, 2, 1])
                xn = sb(ph, "xn", [P, 2, D])
                acc = sb(ph, "acc", [P, 2, 3, D])
                sg_p = [pb(ph, f"sg_p{k}") for k in range(2)]
                t_p = [pb(ph, f"t_p{k}") for k in range(2)]
                s_p = [pb(ph, f"s_p{k}") for k in range(2)]
                s = Names(pool)
                w_in_s, ones_s, pool_go, aggr_go = s.many(4)
                n_in, s_in, c_in, x1_s, st_s, mv_s, ve_s, rs_s, deg_s, tot_s = (s.many(2) for _ in range(10))
                tt_s, tc_s, sp_s, sgm_s, sga_s, o_c, o_s, stored, p_c = (s.many(2) for _ in range(9))

                def staggered(eng, first, second):
                    first(0, 0)
                    with eng.Fori(0, PAIRS - 1) as t:
                        first(t, 1)
                        second(t, 0)
                        first(t + 1, 0)
                        second(t, 1)
                    first(PAIRS - 1, 1)
                    second(PAIRS - 1, 0)
                    second(PAIRS - 1, 1)

                with nc.Block() as block:
                    @block.sync
                    def _(sp):
                        sp.wait_ge(ones_s, 1)
                        sp.dma_start(wsum_s[:, :], w_sum).then_inc(w_in_s, 16)
                        sp.dma_start(bsum_b[:, :], b_sum.rearrange("(a n) -> a n", a=1).to_broadcast([P, D])).then_inc(w_in_s, 16)
                        for j, (w, b) in enumerate(((w_cent, b_cent), (w_vor, b_vor))):
                            sp.dma_start(wb[0:1, j, :], w).then_inc(w_in_s, 16)
                            sp.dma_start(wb[1:2, j, :], b.rearrange("(a n) -> a n", a=1)).then_inc(w_in_s, 16)
                        with sp.Fori(0, PAIRS) as t:
                            for k in range(2):
                                n = t * 2 + k
                                x_n, h_n = rows(x, n), rows(Hd, n)
                                sum_n = [rows(sum_d[r], n) for r in range(TABLES)]
                                vec_n = [vec[bass.ds(n, 1), :] for vec in (cent_v, vor_v)]
                                sp.wait_ge(sgm_s[k], t)
                                for j in range(2):
                                    sp.dma_start(vecs[0:1, k, j, :], vec_n[j]).then_inc(c_in[k], 16)
                                sp.wait_ge(x1_s[k], t)
                                sp.dma_start(xin[:, k, :], x_n).then_inc(n_in[k], 16)
                                sp.dma_start(hin[:, k, :], h_n).then_inc(n_in[k], 16)
                                sp.wait_ge(p_c[k], t * 2)
                                for r in range(TABLES):
                                    sp.dma_start(sin[:, k, r, :], sum_n[r]).then_inc(s_in[k], 16)

                    @block.gpsimd
                    def _(g):
                        def look_up(t, k):
                            g.wait_ge(deg_s[k], t + 1)
                            g.wait_ge(sp_s[k], t)
                            g.sem_inc(pool_go, 1)
                            for j, (buf, table) in enumerate(((zi, z_in), (zo, z_out))):
                                g.indirect_dma_start(out=buf[:, k, :], out_offset=None, in_=table,
                                                     in_offset=bass.IndirectOffsetOnAxis(ap=ideg[:, k, j:j + 1], axis=0)
                                                     ).then_inc(zi_s[k], 16)
                            g.wait_ge(ve_s[k], t + 1)
                            g.tensor_tensor(out=rs[:, k, :], in0=veps[:, k, :], in1=neghalf[:, :], op=ALU.pow).then_inc(rs_s[k], 1)

                        with g.Fori(0, PAIRS) as t:
                            for k in range(2):
                                look_up(t, k)

                    @block.vector
                    def _(v):
                        v.memset(vecs[:, :, :, :], 1.0).then_inc(ones_s, 1)

                        def start(t, k):
                            n = t * 2 + k
                            v.wait_ge(s_in[k], t * 64 + 64)
                            v.wait_ge(tt_s[k], t)
                            v.tensor_tensor(out=pair[:, k, 0, :], in0=sin[:, k, 0, :], in1=sin[:, k, 1, :], op=ALU.add).then_inc(p_c[k], 1)
                            v.tensor_tensor(out=pair[:, k, 1, :], in0=sin[:, k, 2, :], in1=sin[:, k, 3, :], op=ALU.add).then_inc(p_c[k], 1)
                            v.wait_ge(zi_s[k], t * 32)
                            v.tensor_scalar(out=ideg[:, k, 0:1], in0=sums[:, bass.ds(n * XW + D + 2 * H, 1)],
                                            scalar1=float(MAX_DEG), scalar2=None, op0=ALU.min)
                            v.wait_ge(p_c[k], t * 2 + 2)
                            v.tensor_tensor(out=tot[:, k, :], in0=pair[:, k, 0, :], in1=pair[:, k, 1, :], op=ALU.add).then_inc(tot_s[k], 1)
                            v.wait_ge(n_in[k], t * 32 + 32)
                            v.tensor_tensor(out=x1[:, k, :], in0=xin[:, k, :], in1=hin[:, k, :], op=ALU.add).then_inc(x1_s[k], 1)
                            v.wait_ge(tot_s[k], t + 1)
                            v.tensor_scalar(out=ideg[:, k, 1:2], in0=tot[:, k, ED:ED + 1], scalar1=float(MAX_DEG),
                                            scalar2=None, op0=ALU.min).then_inc(deg_s[k], 1)
                            v.wait_ge(x1_s[k], t + 1)
                            v.bn_stats(out=st[:, k, :], in_=x1[:, k, :]).then_inc(st_s[k], 1)
                            v.wait_ge(st_s[k], t + 1)
                            v.sem_inc(aggr_go, 1)
                            v.bn_aggr(out=mv[:, k, :], in_=st[:, k, :]).then_inc(mv_s[k], 1)
                            v.wait_ge(mv_s[k], t + 1)
                            v.tensor_scalar(out=veps[:, k, :], in0=mv[:, k, 1:2], scalar1=EPS, scalar2=None,
                                            op0=ALU.add).then_inc(ve_s[k], 1)

                        def total(t, k):
                            c = t * 3
                            v.wait_ge(rs_s[k], t + 1)
                            v.tensor_scalar(out=xn[:, k, :], in0=x1[:, k, :], scalar1=mv[:, k, 0:1], scalar2=rs[:, k, :],
                                            op0=ALU.subtract, op1=ALU.mult).then_inc(o_c[k], 1)
                            v.wait_ge(sp_s[k], t + 1)
                            v.wait_ge(stored[k], t * 16)
                            v.scalar_tensor_tensor(out=acc[:, k, 0, :], in0=bsum_b[:, :], scalar=tot[:, k, ED:ED + 1],
                                                   in1=s_p[k][:, 0:D], op0=ALU.mult, op1=ALU.add).then_inc(o_c[k], 1)
                            v.wait_ge(o_c[k], c + 1)
                            v.scalar_tensor_tensor(out=acc[:, k, 1, :], in0=xn[:, k, :], scalar=0.0, in1=x1[:, k, :],
                                                   op0=ALU.max, op1=ALU.add).then_inc(o_c[k], 1)
                            v.wait_ge(o_c[k], c + 3)
                            v.tensor_tensor(out=acc[:, k, 2, :], in0=acc[:, k, 0, :], in1=acc[:, k, 1, :], op=ALU.add).then_inc(o_s[k], 1)

                        v.wait_ge(w_in_s, 16 * 6)
                        staggered(v, start, total)

                    @block.scalar
                    def _(a):
                        def begin(t, k):
                            a.wait_ge(tt_s[k], t + 1)
                            a.wait_ge(sp_s[k], t)
                            a.activation(totT[:, k, :], t_p[k][:, 0:P], ACT.Copy).then_inc(tc_s[k], 1)
                            a.wait_ge(sgm_s[k], t + 1)
                            a.activation(sg[:, k, :], sg_p[k][:, :], ACT.Sigmoid).then_inc(sga_s[k], 1)

                        def store(t, k):
                            a.wait_ge(o_s[k], t + 1)
                            a.dma_start(rows(out, t * 2 + k), acc[:, k, 2, :]).then_inc(stored[k], 16)

                        staggered(a, begin, store)
                        for k in range(2):
                            a.wait_ge(stored[k], 16 * PAIRS)

                    @block.tensor
                    def _(pe):
                        pe.wait_ge(w_in_s, 16 * 6)
                        def begin(t, k):
                            pe.wait_ge(c_in[k], t * 32 + 32)
                            pe.wait_ge(sga_s[k], t)
                            for j in range(2):
                                ins = pe.matmul(sg_p[k][:, j * D:(j + 1) * D], vecs[:, k, j, :], wb[:, j, :], start=True, stop=True)
                            ins.then_inc(sgm_s[k], 1)
                            pe.wait_ge(tot_s[k], t + 1)
                            pe.wait_ge(tc_s[k], t)
                            pe.transpose(t_p[k][:, 0:P], tot[:, k, 0:P], ident[:, :]).then_inc(tt_s[k], 1)

                        def attributes(t, k):
                            pe.wait_ge(tc_s[k], t + 1)
                            pe.wait_ge(o_s[k], t)
                            pe.matmul(s_p[k][:, 0:D], totT[:, k, :], wsum_s[:, :], start=True, stop=False)
                            pe.wait_ge(sga_s[k], t + 1)
                            for j in range(2):
                                pe.matmul(s_p[k][:, 0:D], ident[:, :], sg[:, k, j * D:(j + 1) * D], start=False, stop=False)
                            pe.wait_ge(zi_s[k], t * 32 + 32)
                            pe.matmul(s_p[k][:, 0:D], ident[:, :], zi[:, k, :], start=False, stop=False)
                            pe.matmul(s_p[k][:, 0:D], ident[:, :], zo[:, k, :], start=False, stop=True).then_inc(sp_s[k], 1)

                        begin(0, 0)
                        with pe.Fori(0, PAIRS - 1) as t:
                            attributes(t, 0)
                            begin(t, 1)
                            attributes(t, 1)
                            begin(t + 1, 0)
                        attributes(PAIRS - 1, 0)
                        begin(PAIRS - 1, 1)
                        attributes(PAIRS - 1, 1)
                end_phase()

        project(-1)
        for l in range(L):
            with ExitStack() as edges:
                queries = sb(edges, "queries", [P, NT * QW])
                project(l, queries)
                attend(l, queries)
            update(l)
        finish()


def kernel(**inputs):
    import numpy as np
    import concourse.bacc as bacc
    from concourse.bass_utils import run_bass_kernel_spmd as run

    def padded(a, shape, fill=0):
        out = np.full(shape, fill, a.dtype)
        out[tuple(slice(0, n) for n in a.shape)] = a
        return out

    a = {name: np.asarray(v) for name, v in inputs.items()}
    groups = GROUPS + 2
    src, dst = a["src"], a["dst"]
    by_group = padded(src, (groups * EG * P,), N).reshape(groups, P, EG)
    arrays = {
        "x": padded(a["x"], (NPA, D)),
        "src_tiles": padded(src, ((ET + 2) * P,), N).reshape(ET + 2, P),
        "dst_tiles": padded(dst, ((ET + 2) * P,), SENTINEL).reshape(ET + 2, P),
        "src_rows": np.ascontiguousarray(by_group.transpose(0, 2, 1)).reshape(groups, EG * P),
        "src_cols": by_group.reshape(groups * P, EG),
        "edge_attr": padded(a["edge_attr_128"], (groups * EG * P, ED)).reshape(groups * P, EG * ED),
        "vor_v": padded(a["node_vec1"], (NPA, 1)).reshape(NTA, P),
        "cent_v": padded(a["node_vec1_n2"], (NPA, 1)).reshape(NTA, P),
    }
    for name in ("w_in", "b_in", "ln1_g", "ln1_b", "ln2_g", "ln2_b", "wq", "bq", "wk", "bk", "wv", "bv",
                 "wo", "bo", "w1", "b1", "w2", "b2"):
        arrays[name] = np.ascontiguousarray(a[f"L0_gnn_{name}"])
    for name in ("z_in", "z_out", "W_cent", "b_cent", "W_vor", "b_vor", "W_sum", "b_sum"):
        arrays[name] = np.ascontiguousarray(a[f"L1_gnn_{name}"])

    nc = bacc.Bacc("TRN2", target_bir_lowering=False, num_devices=1)
    args = [nc.dram_tensor(f"in_{n}", v.shape, mybir.dt.from_np(v.dtype), kind="ExternalInput").ap()
            for n, v in arrays.items()]
    args.append(nc.dram_tensor("out_0", (NP, D), f32, kind="ExternalOutput").ap())
    gnn_kernel(nc, *args)
    r = run(nc, [{f"in_{n}": v for n, v in arrays.items()}], core_ids=[0])
    return r.results[0]["out_0"][0:N]
```
